# Optimizing a Trainium2 kernel written in Bass

```python
import numpy as np
import jax
import jax.numpy as jnp

def _softmax(x, axis=-1):
    return jax.nn.softmax(x, axis=axis)

def _gelu(x):
    return jax.nn.gelu(x, approximate=True)

def _silu(x):
    return jax.nn.silu(x)

def _sigmoid(x):
    return jax.nn.sigmoid(x)

def _layernorm(x, axis=-1, eps=1e-05):
    m = jnp.mean(x, axis=axis, keepdims=True)
    v = jnp.var(x, axis=axis, keepdims=True)
    return (x - m) / jnp.sqrt(v + eps)

def _scatter_add(tgt, idx, src, axis=0):
    return tgt.at[idx].add(src)

def _segment_sum(src, seg, n):
    return jax.ops.segment_sum(src, seg, n)
kernel_name = 'mk_seq_preln_d1_jaxref_r8_daf3a8'

def setup_inputs(seed: int=0):
    np.random.seed(seed)
    _w = jnp.asarray

    def _L0_attn_setup():
        import jax, jax.numpy as jnp
        import numpy as np
        D_MODEL = 256
        N_HEADS = 16
        HEAD_DIM = D_MODEL // N_HEADS
        WINDOW = 32
        G = 16
        LN_EPS = 1e-05

        def _sparse_mask(T, dtype=jnp.float32):
            i = jnp.arange(T)[:, None]
            j = jnp.arange(T)[None, :]
            band = (j <= i) & (j >= i - WINDOW + 1)
            neg = jnp.array(-jnp.inf, dtype)
            mask = jnp.full((G + T, G + T), neg, dtype)
            mask = mask.at[:G, :].set(0.0)
            mask = mask.at[:, :G].set(0.0)
            mask = mask.at[G:, G:].set(jnp.where(band, jnp.array(0.0, dtype), neg))
            return mask
        key = jax.random.key(seed)
        ks = jax.random.split(key, 6)
        B, T, D = (2, 256, D_MODEL)
        s = 1.0 / np.sqrt(D)
        return {'x': jax.random.normal(ks[0], (B, T, D), jnp.float32), 'global_tokens': jax.random.normal(ks[1], (1, G, D), jnp.float32) * 0.02, 'ln_scale': jnp.ones((D,), jnp.float32), 'ln_bias': jnp.zeros((D,), jnp.float32), 'Wq': jax.random.normal(ks[2], (D, D), jnp.float32) * s, 'Wk': jax.random.normal(ks[3], (D, D), jnp.float32) * s, 'Wv': jax.random.normal(ks[4], (D, D), jnp.float32) * s, 'Wo': jax.random.normal(ks[5], (D, D), jnp.float32) * s}
    _L0_attn_in = _L0_attn_setup()

    def _L0_ffn_setup():
        import jax, jax.numpy as jnp
        import numpy as np
        TOP_K = 6
        CAP_FACTOR = 2

        def _shared_swiglu(x, wg, wu, wd):
            return jax.nn.silu(x @ wg.T) * (x @ wu.T) @ wd.T
        key = jax.random.key(seed)
        ks = jax.random.split(key, 8)
        B, S, D, E, F, FS = (4, 256, 256, 64, 176, 352)
        scale = jnp.float32(0.02)
        return {'hidden_states': jax.random.normal(ks[0], (B, S, D), jnp.float32), 'gate_w': jax.random.normal(ks[1], (E, D), jnp.float32) * scale, 'w_gate': jax.random.normal(ks[2], (E, F, D), jnp.float32) * scale, 'w_up': jax.random.normal(ks[3], (E, F, D), jnp.float32) * scale, 'w_down': jax.random.normal(ks[4], (E, D, F), jnp.float32) * scale, 'sh_gate': jax.random.normal(ks[5], (FS, D), jnp.float32) * scale, 'sh_up': jax.random.normal(ks[6], (FS, D), jnp.float32) * scale, 'sh_down': jax.random.normal(ks[7], (D, FS), jnp.float32) * scale}
    _L0_ffn_in = _L0_ffn_setup()
    _d = {'L0_attn_x': _L0_attn_in['x'], 'L0_attn_global_tokens': _L0_attn_in['global_tokens'], 'L0_attn_ln_scale': _L0_attn_in['ln_scale'], 'L0_attn_ln_bias': _L0_attn_in['ln_bias'], 'L0_attn_Wq': _L0_attn_in['Wq'], 'L0_attn_Wk': _L0_attn_in['Wk'], 'L0_attn_Wv': _L0_attn_in['Wv'], 'L0_attn_Wo': _L0_attn_in['Wo'], 'L0_ffn_gate_w': _L0_ffn_in['gate_w'], 'L0_ffn_w_gate': _L0_ffn_in['w_gate'], 'L0_ffn_w_up': _L0_ffn_in['w_up'], 'L0_ffn_w_down': _L0_ffn_in['w_down'], 'L0_ffn_sh_gate': _L0_ffn_in['sh_gate'], 'L0_ffn_sh_up': _L0_ffn_in['sh_up'], 'L0_ffn_sh_down': _L0_ffn_in['sh_down']}
    _x0 = _d['L0_attn_x']
    _d['L0_attn_x'] = jax.random.normal(jax.random.fold_in(jax.random.key(seed), 1), (1, 2048, 256), dtype=_x0.dtype)
    del _x0
    return _d

def reference(L0_attn_x, L0_attn_global_tokens, L0_attn_ln_scale, L0_attn_ln_bias, L0_attn_Wq, L0_attn_Wk, L0_attn_Wv, L0_attn_Wo, L0_ffn_gate_w, L0_ffn_w_gate, L0_ffn_w_up, L0_ffn_w_down, L0_ffn_sh_gate, L0_ffn_sh_up, L0_ffn_sh_down):

    def _L0_attn_ref(x, global_tokens, ln_scale, ln_bias, Wq, Wk, Wv, Wo):
        import jax, jax.numpy as jnp
        import numpy as np
        D_MODEL = 256
        N_HEADS = 16
        HEAD_DIM = D_MODEL // N_HEADS
        WINDOW = 32
        G = 16
        LN_EPS = 1e-05

        def _sparse_mask(T, dtype=jnp.float32):
            i = jnp.arange(T)[:, None]
            j = jnp.arange(T)[None, :]
            band = (j <= i) & (j >= i - WINDOW + 1)
            neg = jnp.array(-jnp.inf, dtype)
            mask = jnp.full((G + T, G + T), neg, dtype)
            mask = mask.at[:G, :].set(0.0)
            mask = mask.at[:, :G].set(0.0)
            mask = mask.at[G:, G:].set(jnp.where(band, jnp.array(0.0, dtype), neg))
            return mask
        B, T, D = x.shape
        residual = x
        mu = jnp.mean(x, axis=-1, keepdims=True)
        var = jnp.mean(jnp.square(x - mu), axis=-1, keepdims=True)
        xn = (x - mu) * jax.lax.rsqrt(var + LN_EPS) * ln_scale + ln_bias
        g = jnp.broadcast_to(global_tokens, (B, G, D))
        xg = jnp.concatenate([g, xn], axis=1)

        def proj(W):
            return (xg @ W.T).reshape(B, G + T, N_HEADS, HEAD_DIM)
        Q, K, V = (proj(Wq), proj(Wk), proj(Wv))
        scale = HEAD_DIM ** (-0.5)
        scores = jnp.einsum('bqhd,bkhd->bhqk', Q, K) * scale
        scores = scores + _sparse_mask(T, scores.dtype)[None, None]
        attn = jax.nn.softmax(scores, axis=-1)
        out = jnp.einsum('bhqk,bkhd->bqhd', attn, V).reshape(B, G + T, D)
        out = out[:, G:] @ Wo.T
        return out + residual

    def _L0_ffn_ref(hidden_states, gate_w, w_gate, w_up, w_down, sh_gate, sh_up, sh_down):
        import jax, jax.numpy as jnp
        import numpy as np
        TOP_K = 6
        CAP_FACTOR = 2

        def _shared_swiglu(x, wg, wu, wd):
            return jax.nn.silu(x @ wg.T) * (x @ wu.T) @ wd.T
        B, S, D = hidden_states.shape
        E = gate_w.shape[0]
        x = hidden_states.reshape(-1, D)
        N = x.shape[0]
        A = N * TOP_K
        C = CAP_FACTOR * ((A + E - 1) // E)
        scores = jax.nn.softmax(x @ gate_w.T, axis=-1)
        topk_w, topk_idx = jax.lax.top_k(scores, TOP_K)
        topk_w = topk_w / (topk_w.sum(-1, keepdims=True) + 1e-20)
        flat_e = topk_idx.reshape(-1)
        flat_w = topk_w.reshape(-1)
        order = jnp.argsort(flat_e)
        se = flat_e[order]
        st = order // TOP_K
        sw = flat_w[order]
        counts = jnp.bincount(flat_e, length=E)
        offsets = jnp.cumsum(counts) - counts
        pos = jnp.arange(A) - offsets[se]
        valid = pos < C
        pos_c = jnp.minimum(pos, C - 1)
        buf = jnp.zeros((E, C, D), x.dtype).at[se, pos_c].add(jnp.where(valid[:, None], x[st], jnp.zeros((), x.dtype)))
        g = jnp.einsum('ecd,efd->ecf', buf, w_gate)
        u = jnp.einsum('ecd,efd->ecf', buf, w_up)
        eo = jnp.einsum('ecf,edf->ecd', jax.nn.silu(g) * u, w_down)
        gathered = eo[se, pos_c] * (sw * valid.astype(sw.dtype))[:, None]
        y = jnp.zeros_like(x).at[st].add(gathered).reshape(B, S, D)
        return y + _shared_swiglu(hidden_states, sh_gate, sh_up, sh_down)
    x = L0_attn_x
    x = x + _L0_attn_ref(_layernorm(x, axis=-1), L0_attn_global_tokens, L0_attn_ln_scale, L0_attn_ln_bias, L0_attn_Wq, L0_attn_Wk, L0_attn_Wv, L0_attn_Wo)
    x = x + _L0_ffn_ref(_layernorm(x, axis=-1), L0_ffn_gate_w, L0_ffn_w_gate, L0_ffn_w_up, L0_ffn_w_down, L0_ffn_sh_gate, L0_ffn_sh_up, L0_ffn_sh_down)
    return x

_drawn_inputs = setup_inputs


def setup_inputs(seed=0):
    import zlib

    import numpy as np

    out = dict(_drawn_inputs(seed))
    spreads = {'L0_attn_ln_scale': (1.0, 0.2), 'L0_attn_ln_bias': (0.0, 0.1)}
    factors = {'L0_attn_global_tokens': 26.376,
     'L0_ffn_gate_w': 8.0,
     'L0_ffn_w_gate': 8.0,
     'L0_ffn_w_up': 8.0,
     'L0_ffn_w_down': 8.0,
     'L0_ffn_sh_gate': 5.791,
     'L0_ffn_sh_up': 5.729,
     'L0_ffn_sh_down': 5.73}
    for name, (base, spread) in spreads.items():
        noise = np.random.default_rng([zlib.crc32(name.encode()), seed]).standard_normal(out[name].shape)
        drawn = base * np.exp(spread * noise) if base else spread * noise
        out[name] = jnp.asarray(drawn.astype(out[name].dtype))
    for name, factor in factors.items():
        out[name] = (out[name] * factor).astype(out[name].dtype)
    return out
```

```python
from contextlib import ExitStack

import concourse.bass as bass
from concourse import mybir

F32 = mybir.dt.float32
BF16 = mybir.dt.bfloat16
I32 = mybir.dt.int32
U32 = mybir.dt.uint32
ALU = mybir.AluOpType
ACT = mybir.ActivationFunctionType
AX = mybir.AxisListType

P = 128
T, D = 2048, 256
NT = T // P
DC = D // P
H, HD, G, WIN = 16, 16, 16, 32
BLK = 64
NB = P // BLK
WK = WIN + BLK
NK = WK + G
RG = 4
NJ = H // RG
HV = HD + 1
EX, TOPK, F, FS = 64, 6, 176, 352
CAP = 2 * ((T * TOPK + EX - 1) // EX)
MAIN = 256
TPE = CAP // P
FT = F - P
W1C = 2 * P + 64 + FT
META = D
ROW = 280
LN_EPS = 1e-5
SM_SCALE = float(HD) ** -0.5
NEG = -1e30
BIG = 1 << 15
UN = 4
SG = 512


class Step:

    def __init__(self, off, i=None, coef=0):
        self.off, self.i, self.coef = off, i, coef

    def __add__(self, n):
        return Step(self.off + n, self.i, self.coef)

    def __sub__(self, n):
        return self + -n

    def times(self, per, n=0):
        const = per * self.off + n
        return const if self.i is None else self.i * (per * self.coef) + const

    @property
    def odd(self):
        return self.off % 2

    def first(self, n=1):
        return self.i is None and self.off < n


def build(nc, x, glob, ln_s, ln_b, wq, wk, wv, wo, gate, w1, w2, shg, shu, shd, out):
    table = nc.dram_tensor("slot_table", (EX * CAP, 1), I32, kind="Internal").ap()
    rows = nc.dram_tensor("token_rows", (T + 1, ROW), F32, kind="Internal").ap()
    results = nc.dram_tensor("results", (T * TOPK, D), F32, kind="Internal").ap()

    with ExitStack() as ctx:
        def sb(name, shape, dt=F32):
            return ctx.enter_context(nc.sbuf_tensor(name, shape, dt))

        def sem(name):
            return ctx.enter_context(nc.semaphore(name))

        def sem2(name, n=2):
            return [sem(f"{name}{j}") for j in range(n)]

        PS = ctx.enter_context(nc.psum_tensor("PS", [P, 8, 512], F32))

        passed = sem("passed")

        def hold(e, sm, value):
            e.wait_ge(sm, value)
            if not isinstance(value, int):
                e.sem_inc(passed, 1)

        ident = sb("ident", [P, P])
        tri = sb("tri", [P, P], BF16)
        ones = sb("ones", [P, P], BF16)
        mask = sb("mask", [P, 2, NK])
        parity = sb("parity", [P, 2])
        iota_e = sb("iota_e", [P, EX])
        result_row = sb("result_row", [P, NT, TOPK])
        token_id = sb("token_id", [P, NT], I32)
        lns = sb("lns", [P, 2, DC])
        gT = sb("gT", [P, DC, G])
        wq_s, wk_s, wv_s, wo_s = (sb(n, [P, DC, D]) for n in ("wq_s", "wk_s", "wv_s", "wo_s"))
        gate_s = sb("gate_s", [P, DC, EX])
        shg_s = sb("shg_s", [P, DC, FS])
        shu_s = sb("shu_s", [P, DC, FS])
        shd_s = sb("shd_s", [P, 3, D])
        init_i = sb("init_i", [P, EX * CAP // P], I32)
        init_row = sb("init_row", [1, ROW])

        XA = sb("XA", [P, NT, D])
        XN = sb("XN", [P, 2, D])
        stats = sb("stats", [P, NT, 6])
        mv1 = sb("mv1", [P, NT, 2])
        mv2 = sb("mv2", [P, NT, 2])
        rstd1 = sb("rstd1", [P, NT])
        rstd2 = sb("rstd2", [P, NT])
        nv = sb("nv", [P, NT])
        ni = sb("ni", [P, NT], I32)
        ny = sb("ny", [P, NT])
        nt_ = sb("nt_", [P, NT])
        stats3 = sb("stats3", [P, 6])
        mv3 = sb("mv3", [P, 2])
        rstd3 = sb("rstd3", [P, 1])
        xnT = sb("xnT", [P, 2, DC, P])
        QT = sb("QT", [P, 2, 2, DC, P])
        KW = sb("KW", [P, 2, DC, NB, NK])
        VS = sb("VS", [P, 2, H, HV])
        VW = sb("VW", [P, 2, NB, H, HV])
        SM = sb("SM", [P, 2, H, NK])
        smax = sb("smax", [P, H])
        PT = sb("PT", [P, 2, NJ, P])
        rden = sb("rden", [P, H])
        AO = sb("AO", [P, 2, D])
        AOT = sb("AOT", [P, 2, DC, P])
        X1 = sb("X1", [P, NT, D])
        XR = sb("XR", [P, 2, ROW])
        X2T = sb("X2T", [P, 2, DC, P])
        X2all = sb("X2all", [P, DC, T])
        gmax = sb("gmax", [P, 1])
        gexp = sb("gexp", [P, EX])
        gsum = sb("gsum", [P, 1])
        ginv = sb("ginv", [P, 1])
        top = sb("top", [P, 8])
        topi = sb("topi", [P, 8], U32)
        wsum = sb("wsum", [P, 1])
        winv = sb("winv", [P, 1])
        hot = sb("hot", [P, TOPK, EX])
        hotp = sb("hotp", [P, TOPK, EX])
        M = sb("M", [P, EX], BF16)
        Macc = sb("Macc", [P, EX], BF16)
        pos = sb("pos", [P, TOPK])
        over = sb("over", [P, TOPK])
        slotf = sb("slotf", [P, TOPK])
        slot = sb("slot", [P, 2, TOPK], I32)
        tid = sb("tid", [P, 2], I32)
        cmaxf = sb("cmaxf", [P, 1])
        cmax = sb("cmax", [P, 1], I32)
        SS = sb("SS", [P, 2, SG])
        SH = sb("SH", [P, 3, SG])
        NTAB = EX * TPE // 2
        tabi = sb("tabi", [NTAB, 2, P], I32)
        tabf = sb("tabf", [NTAB, 2, P])
        tabT = sb("tabT", [P, EX, TPE])
        gidx = sb("gidx", [P, UN, 2], I32)
        W1 = sb("W1", [P, UN, DC, W1C])
        W2 = sb("W2", [P, UN, 2, D])
        XG = sb("XG", [P, UN, 2, ROW])
        XET = sb("XET", [P, 2, DC, MAIN])
        hit = sb("hit", [P, 2, TOPK])
        hitw = sb("hitw", [P, 2, TOPK])
        hitr = sb("hitr", [P, 2, TOPK])
        wsel = sb("wsel", [P, UN, 2])
        rsel = sb("rsel", [P, 2])
        dest = sb("dest", [P, UN, 2], I32)
        SL = sb("SL", [P, 2, 2, MAIN])
        HE = sb("HE", [P, 2, 2, MAIN])
        YE = sb("YE", [P, UN, 2, D])
        YT = sb("YT", [P, 2, TOPK, D])
        YS = sb("YS", [P, 2, D])
        OUT = sb("OUT", [P, 2, D])
        zero = sb("zero", [P, 2048])

        w_loaded = sem("w_loaded")
        sh_loaded = sem("sh_loaded")
        init_done = sem("init_done")
        dconst = sem("dconst")
        table_init = sem("table_init")
        glob_done, glob_evac = sem("glob_done"), sem("glob_evac")
        x_loaded = sem2("x_loaded", 4)
        dve_0 = sem("dve_0")
        dve_b, dve_c = sem("dve_b"), sem("dve_c")
        stat1, stat2 = sem("stat1"), sem("stat2")
        xa_ready, xn_ready, res_ready = sem("xa_ready"), sem("xn_ready"), sem("res_ready")
        xt_done, xt_evac = sem("xt_done"), sem("xt_evac")
        qk_done, v_done = sem("qk_done"), sem("v_done")
        qk_evac, v_evac = sem("qk_evac"), sem("v_evac")
        vw_loaded = sem2("vw_loaded")
        s_done, s_read = sem("s_done"), sem("s_read")
        sub_ready, exp_ready = sem("sub_ready"), sem("exp_ready")
        pt_done, pt_evac, pv_done = sem("pt_done"), sem("pt_evac"), sem("pv_done")
        ao_ready = sem("ao_ready")
        aot_done, aot_evac = sem("aot_done"), sem("aot_evac")
        wo_done, x1_ready, x2_ready = sem("wo_done"), sem("x1_ready"), sem("x2_ready")
        x2t_done, x2t_evac = sem("x2t_done"), sem("x2t_evac")
        gate_done, gmax_ready, gexp_ready = sem("gate_done"), sem("gmax_ready"), sem("gexp_ready")
        row_ready, row_stored = sem("row_ready"), sem2("row_stored")
        m_ready, pos_done = sem("m_ready"), sem("pos_done")
        slot_ready, slot_stored = sem("slot_ready"), sem2("slot_stored")
        cnt_done, cmax_ready = sem("cnt_done"), sem("cmax_ready")
        routed = sem("routed")
        sh_done, sh_silu, sh_mul = sem("sh_done"), sem("sh_silu"), sem("sh_mul")
        shd_done, sh_add = sem("shd_done"), sem("sh_add")
        tab_loaded, tab_f, tab_t, tab_ready = sem("tab_loaded"), sem("tab_f"), sem("tab_t"), sem("tab_ready")
        zeroed = sem("zeroed")
        ew_loaded = sem2("ew_loaded", UN)
        idx_ready = sem("idx_ready")
        xg_loaded = sem2("xg_loaded", UN)
        dve_e = sem("dve_e")
        et_done, et_evac = sem("et_done"), sem("et_evac")
        gu_done, gt_done = sem("gu_done"), sem("gt_done")
        silu_ready, h_ready = sem("silu_ready"), sem("h_ready")
        dn_done, y_ready = sem("dn_done"), sem("y_ready")
        y_stored = sem2("y_stored", UN)
        all_stored = sem("all_stored")
        yt_loaded = sem2("yt_loaded")
        cst, idx_free = sem("cst"), sem("idx_free")
        ysum, out_ready = sem("ysum"), sem("out_ready")
        out_stored = sem2("out_stored")

        S_ps = PS[:, 0:4, 0:NJ * NK].rearrange("p g (j k) -> p g j k", j=NJ)
        SM_v = SM[:, :, :, :].rearrange("p t (g j) k -> p t g j k", g=RG)
        PT_ps = PS[0:NK, 0:4, :].rearrange("p g (j q) -> p g j q", j=NJ)
        AOT_ps = PS[:, 4, 0:D].rearrange("p (c q) -> p c q", c=DC)
        X2T_ps = PS[:, 4, D:2 * D].rearrange("p (c q) -> p c q", c=DC)
        XT_ps = PS[:, 5, 0:D].rearrange("p (c q) -> p c q", c=DC)
        V_ps = PS[:, 5, D:2 * D]
        O_ps = PS[:, 5, 0:H * HV].rearrange("p (h v) -> p h v", h=H)
        WO_ps = PS[:, 6, 0:D]
        gate_ps = PS[:, 6, D:D + EX]
        pos_ps = PS[:, 6, D + EX:D + 2 * EX]
        cnt_ps = PS[:, 6, D + 2 * EX:D + 3 * EX]
        Q_ps = PS[:, 7, 0:D].rearrange("p (c q) -> p c q", c=DC)
        K_ps = PS[:, 7, D:2 * D].rearrange("p (c q) -> p c q", c=DC)

        def head(g, j):
            return 8 * (j // 2) + 2 * g + j % 2

        def steps(engine, step):
            step(Step(0))
            step(Step(1))
            with engine.Fori(0, NT // 2 - 1) as i:
                step(Step(2, i, 2))
                step(Step(3, i, 2))
            step(Step(NT))
            step(Step(NT + 1))

        def before(e, base, per):
            return e.i * (per * UN) + per * max(base + e.off - 1, 0)

        def has_a(s):
            return s.i is not None or s.off < NT

        def has_b(s):
            return s.i is not None or 1 <= s.off <= NT

        def has_c(s):
            return s.i is not None or s.off >= 2

        NW = 8

        NBS, NC, NE = 5, 30, 5

        ctx.enter_context(nc.allow_low_precision(reason="whole numbers up to 16"))
        block = ctx.enter_context(nc.Block())

        @block.sync
        def _(sp):
            for q in range(4):
                n = NT // 4
                sp.dma_start(X1[:, q * n:(q + 1) * n, :], x[q * n * P:(q + 1) * n * P, :].rearrange("(t p) d -> p t d", p=P))\
                  .then_inc(x_loaded[q], 16)
            chunk = "(c p) n -> p c n"
            sp.dma_start(lns[:, 0, :], ln_s).then_inc(w_loaded, 16)
            sp.dma_start(lns[:, 1, :], ln_b).then_inc(w_loaded, 16)
            for dst, src in ((wq_s, wq), (wk_s, wk), (wv_s, wv), (gT, glob), (wo_s, wo), (gate_s, gate)):
                sp.dma_start(dst[:, :, :], src.rearrange(chunk, p=P)).then_inc(w_loaded, 16)
            sp.dma_start(shg_s[:, :, :], shg.rearrange(chunk, p=P)).then_inc(sh_loaded, 16)
            sp.wait_ge(init_done, 1)
            sp.dma_start(table.rearrange("(p n) o -> p (n o)", p=P), init_i[:, :]).then_inc(table_init, 16)
            sp.dma_start(rows[T:T + 1, :], init_row[:, :]).then_inc(table_init, 16)

            def step(s):
                if has_a(s):
                    hold(sp, v_evac, s.times(1, 1))
                    if not s.first(2):
                        hold(sp, pv_done, s.times(RG, -RG))
                    sp.dma_start(VW[WIN:WK, s.odd, 0], VS[0:BLK, s.odd]).then_inc(vw_loaded[s.odd], 16)
                    sp.dma_start(VW[0:WK, s.odd, 1], VS[BLK - WIN:P, s.odd]).then_inc(vw_loaded[s.odd], 16)
                    if not s.first():
                        sp.dma_start(VW[0:WIN, s.odd, 0], VS[P - WIN:P, 1 - s.odd]).then_inc(vw_loaded[s.odd], 16)
                if has_c(s):
                    c = s - 2
                    hold(sp, row_ready, c.times(1, 1))
                    sp.dma_start(rows[bass.ds(c.times(P), P), :], XR[:, c.odd, :]).then_inc(row_stored[c.odd], 16)

            steps(sp, step)

            sp.wait_ge(routed, 1)
            sp.dma_start(tabi[:, :, :], table.rearrange("(c r s) o -> r c (s o)", c=2, s=P)).then_inc(tab_loaded, 16)
            sp.wait_ge(cmax_ready, 1)
            most = sp.value_load(cmax[0:1, 0:1], min_val=0, max_val=T)
            with sp.If(most > CAP):
                n = 2048
                v = results.rearrange("(a p r) d -> a p (r d)", p=P, r=n // D)
                for a in range(v.shape[0]):
                    sp.dma_start(v[a], zero[:, :]).then_inc(zeroed, 16)
                sp.wait_ge(zeroed, 16 * v.shape[0])
                sp.sem_inc(all_stored, 1)
            with sp.Else():
                sp.sem_inc(all_stored, 1)

            def weights(e, j):
                sp.dma_start(W1[:, j], w1[bass.ds(e, 1)].rearrange("e p c n -> p (e c) n")).then_inc(ew_loaded[j], 16)
                sp.dma_start(W2[:, j, 0, :], w2[bass.ds(e, 1), 0:P].rearrange("e p n -> p (e n)")).then_inc(ew_loaded[j], 16)
                sp.dma_start(W2[0:FT, j, 1, :], w2[bass.ds(e, 1), P:F].rearrange("e p n -> p (e n)")).then_inc(ew_loaded[j], 16)

            for j in range(UN):
                weights(j, j)
            with sp.Fori(0, EX // UN - 1) as i:
                for j in range(UN):
                    hold(sp, dn_done, i * UN + (j + 1))
                    e = i * UN + (j + UN)
                    weights(e, j)
            with sp.If(most > MAIN):
                with sp.Fori(0, EX // UN) as i:
                    for j in range(UN):
                        hold(sp, dn_done, i * UN + (EX - UN + j + 1))
                        e = i * UN + j
                        weights(e, j)
                sp.wait_ge(ew_loaded[0], 48)
            with sp.Else():
                sp.wait_ge(ew_loaded[0], 48)

            sp.wait_ge(all_stored, 2)
            res_v = results.rearrange("(t k) d -> t (k d)", k=TOPK)

            def results_in(s):
                if not s.first(2):
                    hold(sp, ysum, s.times(1, -1))
                sp.dma_start(YT[:, s.odd].rearrange("p k d -> p (k d)"),
                             res_v[bass.ds(s.times(P), P), :]).then_inc(yt_loaded[s.odd], 16)

            results_in(Step(0))
            results_in(Step(1))
            with sp.Fori(0, NT // 2 - 1) as i:
                results_in(Step(2, i, 2))
                results_in(Step(3, i, 2))

        @block.tensor
        def _(pe):
            pe.wait_ge(w_loaded, 16 * NW)
            pe.wait_ge(init_done, 1)
            for c in range(DC):
                for d in range(DC):
                    pe.matmul(PS[:, 6, c * G:(c + 1) * G], wk_s[:, d, c * P:(c + 1) * P], gT[:, d, :],
                              start=(d == 0), stop=(d == DC - 1))
            for d in range(DC):
                mm = pe.matmul(PS[WK:NK, 7, 0:D], gT[:, d, :], wv_s[:, d, :], start=(d == 0), stop=(d == DC - 1),
                               tile_position=(0, WK))
            mm.then_inc(glob_done, 1)

            def scores(b):
                pe.wait_ge(qk_evac, b.times(1, 1))
                if not b.first():
                    pe.wait_ge(pt_evac, b.times(RG))
                for j in range(NJ):
                    for g in range(RG):
                        for k in range(NB):
                            r = slice(32 * g, 32 * g + 32)
                            mm = pe.matmul(S_ps[k * BLK:(k + 1) * BLK, g, j, :],
                                           QT[r, b.odd, j % 2, j // 2, k * BLK:(k + 1) * BLK],
                                           KW[r, b.odd, j // 2, k, :], start=True, stop=True)
                mm.then_inc(s_done, 1)

            def step(s):
                a, b, c = s, s - 1, s - 2
                if has_b(s):
                    scores(b)
                if has_c(s):
                    pe.wait_ge(ao_ready, c.times(1, 1))
                    if not c.first():
                        pe.wait_ge(x2t_evac, c.times(1))
                    for k in range(DC):
                        mm = pe.transpose(AOT_ps[:, k, :], AO[:, c.odd, k * P:(k + 1) * P], ident[:, :])
                    mm.then_inc(aot_done, 1)
                if has_a(s):
                    pe.wait_ge(xn_ready, a.times(1, 1))
                    if s.first():
                        pe.wait_ge(glob_evac, 1)
                    if not s.first():
                        pe.wait_ge(v_evac, a.times(1))
                    for k in range(DC):
                        mm = pe.transpose(XT_ps[:, k, :], XN[:, a.odd, k * P:(k + 1) * P], ident[:, :])
                    mm.then_inc(xt_done, 1)
                if has_c(s):
                    pe.wait_ge(aot_evac, c.times(1, 1))
                    if not c.first():
                        pe.wait_ge(slot_ready, c.times(1))
                    for k in range(DC):
                        mm = pe.matmul(WO_ps, AOT[:, c.odd, k, :], wo_s[:, k, :], start=(k == 0), stop=(k == DC - 1))
                    mm.then_inc(wo_done, 1)
                if has_a(s):
                    pe.wait_ge(xt_evac, a.times(1, 1))
                    if not s.first():
                        pe.wait_ge(qk_evac, a.times(1))
                    for ps, w in ((Q_ps, wq_s), (K_ps, wk_s)):
                        for k in range(DC):
                            for d in range(DC):
                                mm = pe.matmul(ps[:, k, :], w[:, d, k * P:(k + 1) * P], xnT[:, a.odd, d, :],
                                               start=(d == 0), stop=(d == DC - 1))
                    mm.then_inc(qk_done, 1)
                    for d in range(DC):
                        mm = pe.matmul(V_ps, xnT[:, a.odd, d, :], wv_s[:, d, :], start=(d == 0), stop=(d == DC - 1))
                    mm.then_inc(v_done, 1)
                if has_c(s):
                    pe.wait_ge(x2_ready, c.times(1, 1))
                    for k in range(DC):
                        mm = pe.transpose(X2T_ps[:, k, :], XR[:, c.odd, k * P:(k + 1) * P], ident[:, :])
                    mm.then_inc(x2t_done, 1)
                    pe.wait_ge(x2t_evac, c.times(1, 1))
                    pe.wait_ge(x1_ready, c.times(1, 1))
                    for k in range(DC):
                        mm = pe.matmul(gate_ps, X2T[:, c.odd, k, :], gate_s[:, k, :], start=(k == 0), stop=(k == DC - 1))
                    mm.then_inc(gate_done, 1)
                if has_b(s):
                    def transposes(n):
                        pe.wait_ge(exp_ready, b.times(2, 1 + n // 2))
                        for k in range(NJ):
                            mm = pe.transpose(PT_ps[:, n, k, :], SM[:, b.odd, NJ * n + k, :], ident[:, :])
                        mm.then_inc(pt_done, 1)

                    def values(n):
                        pe.wait_ge(pt_evac, b.times(RG, n + 1))
                        if n == 0:
                            lo = 48 * (b.off // 2) + 48 - (0 if b.odd else 16)
                            pe.wait_ge(vw_loaded[b.odd], lo if b.i is None else b.i * 48 + lo)
                            pe.wait_ge(v_evac, min(b.off + 2, NT) if b.i is None else b.times(1, 2))
                        for k in range(NJ):
                            h = head(n, k)
                            for q in range(NB):
                                mm = pe.matmul(O_ps[q * BLK:(q + 1) * BLK, h, :],
                                               PT[0:NK, n % 2, k, q * BLK:(q + 1) * BLK],
                                               VW[0:NK, b.odd, q, h, :], start=True, stop=True)
                        mm.then_inc(pv_done, 1)

                    for n in range(RG):
                        transposes(n)
                    for n in range(RG):
                        values(n)
                if has_c(s):
                    pe.wait_ge(m_ready, c.times(1, 1))
                    pe.wait_ge(gexp_ready, c.times(1, 1))
                    pe.matmul(pos_ps, tri[:, :], M[:, :], start=True, stop=False)
                    pe.matmul(pos_ps, ones[:, :], Macc[:, :], start=False, stop=True).then_inc(pos_done, 1)

            steps(pe, step)

            pe.wait_ge(slot_ready, NT)
            pe.matmul(cnt_ps, ones[:, :], Macc[:, :], start=True, stop=True).then_inc(cnt_done, 1)

            pe.wait_ge(sh_loaded, 16 * 4)

            def shared(g):
                for f in range(3):
                    fw = min(P, FS - f * P)
                    n = 3 * 1
                    if g.first() and f < 2:
                        pass
                    else:
                        pe.wait_ge(sh_mul, g.times(3, f - 1))
                    par = f % 2
                    for u, w in enumerate((shg_s, shu_s)):
                        for d in range(DC):
                            mm = pe.matmul(PS[0:fw, 2 * par + u, :], w[:, d, f * P:f * P + fw],
                                           X2all[:, d, bass.ds(g.times(SG), SG)], start=(d == 0), stop=(d == DC - 1))
                    mm.then_inc(sh_done, 1)
                pe.wait_ge(sh_mul, g.times(3, 3))
                for t in range(SG // P):
                    if not (g.first() and t < 2):
                        pe.wait_ge(sh_add, g.times(SG // P, t - 1))
                    for f in range(3):
                        fw = min(P, FS - f * P)
                        mm = pe.matmul(PS[:, 4 + t % 2, 0:D], SH[0:fw, f, t * P:(t + 1) * P], shd_s[0:fw, f, :],
                                       start=(f == 0), stop=(f == 2))
                    mm.then_inc(shd_done, 1)

            pe.wait_ge(cmax_ready, 1)
            shared(Step(0))
            with pe.Fori(0, T // SG - 1) as i:
                shared(Step(1, i, 1))

            pe.wait_ge(tab_f, 1)
            for k in range(2):
                mm = pe.transpose(PS[:, 6, k * NTAB:(k + 1) * NTAB], tabf[:, k, :], ident[0:NTAB, 0:NTAB])
            mm.then_inc(tab_t, 1)
            pe.wait_ge(tab_ready, 1)
            pe.wait_ge(sh_add, NT)
            most = pe.value_load(cmax[0:1, 0:1], min_val=0, max_val=T)

            def rows_t(e, base, nt, j):
                q = j % 2
                pe.wait_ge(xg_loaded[j], e.i * (16 * nt) + (16 * nt + base * 32 // UN) if e.i is not None else 16 * nt)
                pe.wait_ge(et_evac, before(e, base, 1))
                for t in range(nt):
                    for d in range(DC):
                        mm = pe.transpose(PS[:, q, d * MAIN + t * P:d * MAIN + (t + 1) * P],
                                          XG[:, j, t, d * P:(d + 1) * P], ident[:, :])
                mm.then_inc(et_done, 1)

            def expert(e, base, nt, j):
                q = j % 2
                n = nt * P
                pe.wait_ge(ew_loaded[j], e.i * 48 + (48 + base * 48 // UN))
                pe.wait_ge(et_evac, e.times(1, base + 1))
                pe.wait_ge(h_ready, before(e, base, 2))
                for u in range(2):
                    for d in range(DC):
                        mm = pe.matmul(PS[:, 2 + q, u * MAIN:u * MAIN + n], W1[:, j, d, u * P:(u + 1) * P],
                                       XET[:, q, d, 0:n], start=(d == 0), stop=(d == DC - 1))
                mm.then_inc(gu_done, 1)
                pe.wait_ge(h_ready, e.i * (2 * UN) + 2 * (base + j))
                for d in range(DC):
                    mm = pe.matmul(PS[0:W1C - 2 * P, 4, 0:n], W1[:, j, d, 2 * P:W1C], XET[:, q, d, 0:n],
                                   start=(d == 0), stop=(d == DC - 1))
                mm.then_inc(gt_done, 1)

            def down(e, base, nt, j):
                q = j % 2
                pe.wait_ge(h_ready, e.i * (2 * UN) + 2 * (base + j + 1))
                pe.wait_ge(y_ready, before(e, base, 1))
                for t in range(nt):
                    pe.matmul(PS[:, 5 + q, t * D:(t + 1) * D], HE[:, q, 0, t * P:(t + 1) * P], W2[:, j, 0, :],
                              start=True, stop=False)
                    mm = pe.matmul(PS[:, 5 + q, t * D:(t + 1) * D], HE[0:FT, q, 1, t * P:(t + 1) * P],
                                   W2[0:FT, j, 1, :], start=False, stop=True)
                mm.then_inc(dn_done, 1)

            def experts(base, nt):
                with pe.Fori(0, EX // UN) as i:
                    for j in range(UN):
                        e = Step(j, i, UN)
                        rows_t(e, base, nt, j)
                        expert(e, base, nt, j)
                        down(e, base, nt, j)

            experts(0, MAIN // P)
            with pe.If(most > MAIN):
                experts(EX, TPE - MAIN // P)
                pe.wait_ge(tab_ready, 1)
            with pe.Else():
                pe.wait_ge(tab_ready, 1)

        @block.scalar
        def _(act):
            act.dma_start(shu_s[:, :, :], shu.rearrange("(c p) n -> p c n", p=P)).then_inc(sh_loaded, 16)
            act.dma_start(shd_s[:, 0:2, :], shd[0:2 * P, :].rearrange("(c p) n -> p c n", p=P)).then_inc(sh_loaded, 16)
            act.dma_start(shd_s[0:FS - 2 * P, 2, :], shd[2 * P:FS, :]).then_inc(sh_loaded, 16)
            act.wait_ge(w_loaded, 16 * NW)
            act.wait_ge(dconst, 2)
            act.wait_ge(glob_done, 1)
            gk = PS[:, 6, 0:DC * G].rearrange("p (c g) -> p c g", c=DC)
            for t in range(2):
                for k in range(NB):
                    act.copy(KW[:, t, :, k, WK:NK], gk)
                    a = act.copy(VW[WK:NK, t, k, :, 0:HD], PS[WK:NK, 7, 0:D].rearrange("p (h v) -> p h v", h=H))
            a.then_inc(glob_evac, 1)

            def step(s):
                a, b, c = s, s - 1, s - 2
                if has_c(s):
                    act.wait_ge(aot_done, c.times(1, 1))
                    act.copy(AOT[:, c.odd], AOT_ps).then_inc(aot_evac, 1)
                if has_a(s):
                    act.wait_ge(xt_done, a.times(1, 1))
                    if not s.first(2):
                        act.wait_ge(v_done, a.times(1, -1))
                    for d in range(DC):
                        i = act.activation(xnT[:, a.odd, d, :], XT_ps[:, d, :], ACT.Identity,
                                           bias=lns[:, 1, d:d + 1], scale=lns[:, 0, d:d + 1])
                    i.then_inc(xt_evac, 1)
                    act.wait_ge(qk_done, a.times(1, 1))
                    if not s.first(2):
                        act.wait_ge(s_done, a.times(1, -1))
                    for e in range(2):
                        act.mul(QT[:, a.odd, e], Q_ps, parity[:, e:e + 1])
                    if s.first():
                        act.copy(KW[:, 0, :, 0, 0:WIN], KW[:, 1, :, 1, WK - WIN:WK])
                    else:
                        act.wait_ge(qk_evac, a.times(1))
                        act.copy(KW[:, a.odd, :, 0, 0:WIN], KW[:, 1 - a.odd, :, 1, WK - WIN:WK])
                    act.copy(KW[:, a.odd, :, 0, WIN:WK], K_ps[:, :, 0:BLK])
                    act.copy(KW[:, a.odd, :, 1, 0:WK], K_ps[:, :, BLK - WIN:P]).then_inc(qk_evac, 1)
                    act.wait_ge(v_done, a.times(1, 1))
                    if not s.first(2):
                        p = a - 1
                        lo = 48 * (p.off // 2) + 48 - (0 if p.odd else 16)
                        act.wait_ge(vw_loaded[p.odd], lo if p.i is None else p.i * 48 + lo)
                    act.copy(VS[:, a.odd, :, 0:HD], V_ps.rearrange("p (h v) -> p h v", h=H)).then_inc(v_evac, 1)
                if has_b(s):
                    act.wait_ge(sub_ready, b.times(2, 1))
                    act.activation(SM[:, b.odd, 0:H // 2], SM[:, b.odd, 0:H // 2], ACT.Exp,
                                   scale=SM_SCALE).then_inc(exp_ready, 1)
                if has_c(s):
                    act.wait_ge(x2t_done, c.times(1, 1))
                    act.copy(X2T[:, c.odd], X2T_ps)
                    act.copy(X2all[:, :, bass.ds(c.times(P), P)], X2T_ps).then_inc(x2t_evac, 1)
                if has_b(s):
                    act.wait_ge(sub_ready, b.times(2, 2))
                    act.activation(SM[:, b.odd, H // 2:H], SM[:, b.odd, H // 2:H], ACT.Exp,
                                   scale=SM_SCALE).then_inc(exp_ready, 1)
                if has_c(s):
                    act.wait_ge(gmax_ready, c.times(1, 1))
                    act.activation(gexp[:, :], gate_ps, ACT.Exp, bias=gmax[:, 0:1],
                                   accum_out=gsum[:, 0:1]).then_inc(gexp_ready, 1)
                if has_b(s):
                    for n in range(RG):
                        act.wait_ge(pt_done, b.times(RG, n + 1))
                        if not (b.first() and n < 2):
                            act.wait_ge(pv_done, b.times(RG, n - 1))
                        act.copy(PT[0:NK, n % 2], PT_ps[:, n]).then_inc(pt_evac, 1)

            steps(act, step)

            def shared(g):
                for f in range(3):
                    fw = min(P, FS - f * P)
                    act.wait_ge(sh_done, g.times(3, f + 1))
                    if not (g.first() and f < 2):
                        act.wait_ge(sh_mul, g.times(3, f - 1))
                    act.activation(SS[0:fw, f % 2, :], PS[0:fw, 2 * (f % 2), :], ACT.Silu).then_inc(sh_silu, 1)

            shared(Step(0))
            with act.Fori(0, T // SG - 1) as i:
                shared(Step(1, i, 1))

            act.wait_ge(cmax_ready, 1)
            most = act.value_load(cmax[0:1, 0:1], min_val=0, max_val=T)

            def weighted(e, base, nt, j):
                q = j % 2
                act.wait_ge(dn_done, e.times(1, base + 1))
                act.wait_ge(idx_ready, e.times(1, base + 1))
                if base:
                    act.wait_ge(y_stored[j], e.i * (16 * nt) + base // UN * 32)
                else:
                    act.wait_ge(y_stored[j], e.i * (16 * nt))
                for t in range(nt):
                    i = act.mul(YE[:, j, t, :], PS[:, 5 + q, t * D:(t + 1) * D], wsel[:, j, t:t + 1])
                i.then_inc(y_ready, 1)

            def experts(base, nt):
                n = nt * P
                with act.Fori(0, EX // UN) as i:
                    for j in range(UN):
                        e = Step(j, i, UN)
                        q = j % 2
                        act.wait_ge(gu_done, e.times(1, base + 1))
                        act.wait_ge(h_ready, before(e, base, 2))
                        act.activation(SL[:, q, 0, 0:n], PS[:, 2 + q, 0:n], ACT.Silu).then_inc(silu_ready, 1)
                        act.wait_ge(gt_done, e.times(1, base + 1))
                        act.activation(SL[0:FT, q, 1, 0:n], PS[0:FT, 4, 0:n], ACT.Silu).then_inc(silu_ready, 1)
                        weighted(e, base, nt, j)

            experts(0, MAIN // P)
            with act.If(most > MAIN):
                experts(EX, TPE - MAIN // P)
                act.wait_ge(cmax_ready, 1)
            with act.Else():
                act.wait_ge(cmax_ready, 1)

            def store(s):
                act.wait_ge(out_ready, s.times(1, 1))
                act.dma_start(out[bass.ds(s.times(P), P), :], OUT[:, s.odd, :]).then_inc(out_stored[s.odd], 16)

            with act.Fori(0, NT // 2) as i:
                store(Step(0, i, 2))
                store(Step(1, i, 2))
            for t in range(2):
                act.wait_ge(out_stored[t], 16 * NT // 2)

        @block.vector
        def _(dve):
            dve.memset(VS[:, :, :, HD:HV], 1.0)
            dve.memset(VW[:, :, :, :, :], 1.0)
            dve.memset(KW[:, :, :, :, :], 0.0)
            dve.memset(Macc[:, :], 0.0)
            dve.memset(XR[:, :, :], 0.0)
            dve.memset(ones[:, :], 1.0).then_inc(dconst, 1)
            dve.wait_ge(init_done, 1)
            dve.tensor_reduce(parity[:, :], ident[:, :].rearrange("p (b e d) -> p e b d", e=2, d=HD), AX.XY, ALU.add)\
               .then_inc(dconst, 1)
            dve.wait_ge(dconst, 2)

            class Chain:

                def __init__(self, sem, s, per, base=0):
                    self.sem, self.s, self.per, self.n, self.base = sem, s, per, 0, base

                def __call__(self, ins, held=False):
                    self.n += 1
                    ins.then_inc(self.sem, 1)
                    value = self.s.times(self.per, self.base + self.n)
                    if held:
                        hold(dve, self.sem, value)
                    else:
                        dve.wait_ge(self.sem, value)

                def end(self):
                    assert self.n == self.per, (self.n, self.per)

            def rsqrt(link, dst, var, n):
                v, y, t, b = nv[:, 0:n], ny[:, 0:n], nt_[:, 0:n], ni[:, 0:n]
                link(dve.tensor_scalar(v, var, LN_EPS, None, ALU.add))
                link(dve.tensor_scalar(b, v.bitcast(I32), 1, None, ALU.logical_shift_right))
                link(dve.tensor_scalar(y.bitcast(I32), b, -1.0, float(0x5F3759DF), ALU.mult, ALU.add))
                link(dve.tensor_scalar(v, v, -0.5, None, ALU.mult))
                for k in range(3):
                    link(dve.tensor_tensor(t, y, y, ALU.mult))
                    link(dve.tensor_tensor(t, t, v, ALU.mult))
                    link(dve.scalar_tensor_tensor(out=dst if k == 2 else y, in0=t, scalar=1.5, in1=y,
                                                  op0=ALU.add, op1=ALU.mult))

            link0 = Chain(dve_0, Step(0), 0)
            for t in range(NT):
                if t % (NT // 4) == 0:
                    dve.wait_ge(x_loaded[t // (NT // 4)], 16)
                dve.bn_stats(stats[:, t, :], X1[:, t, :]).then_inc(stat1, 1)
            dve.wait_ge(stat1, NT)
            for t in range(NT):
                dve.bn_aggr(mv1[:, t, :], stats[:, t, :]).then_inc(stat1, 1)
            dve.wait_ge(stat1, 2 * NT)
            rsqrt(link0, rstd1[:, :], mv1[:, :, 1], NT)
            for t in range(NT):
                dve.tensor_scalar(XA[:, t, :], X1[:, t, :], mv1[:, t, 0:1], rstd1[:, t:t + 1], ALU.subtract, ALU.mult)\
                   .then_inc(xa_ready, 1)
            for t in range(NT):
                dve.wait_ge(xa_ready, t + 1)
                dve.bn_stats(stats[:, t, :], XA[:, t, :]).then_inc(stat2, 1)
            dve.wait_ge(stat2, NT)
            for t in range(NT):
                dve.bn_aggr(mv2[:, t, :], stats[:, t, :]).then_inc(stat2, 1)
            dve.wait_ge(stat2, 2 * NT)
            rsqrt(link0, rstd2[:, :], mv2[:, :, 1], NT)

            def layernorm(link, dst, src):
                link(dve.bn_stats(stats3[:, :], src), held=True)
                link(dve.bn_aggr(mv3[:, :], stats3[:, :]))
                rsqrt(link, rstd3[:, :], mv3[:, 1:2], 1)
                return dve.tensor_scalar(dst, src, mv3[:, 0:1], rstd3[:, 0:1], ALU.subtract, ALU.mult)

            def softmax_half(link, b, k):
                g = slice(2 * k, 2 * k + 2)
                sm = SM_v[:, b.odd, g]
                mk = mask[:, 0 if b.first() else 1, :]
                if k == 0:
                    dve.wait_ge(s_done, b.times(1, 1))
                    if not b.first(2):
                        dve.wait_ge(pt_done, b.times(RG, -RG))
                for gg in range(2):
                    i = dve.tensor_tensor(SM_v[:, b.odd, 2 * k + gg], S_ps[:, 2 * k + gg],
                                          mk.unsqueeze(1).broadcast_to([P, NJ, NK]), ALU.add)
                    if gg:
                        i.then_inc(s_read, 1)
                    else:
                        link(i)
                dve.wait_ge(s_read, b.times(2, k + 1))
                h = slice(8 * k, 8 * k + 8)
                link(dve.tensor_reduce(smax[:, h], SM[:, b.odd, h, :], AX.X, ALU.max))
                dve.tensor_tensor(SM[:, b.odd, h, :], SM[:, b.odd, h, :],
                                  smax[:, h].unsqueeze(2).broadcast_to([P, 8, NK]), ALU.subtract).then_inc(sub_ready, 1)
                dve.wait_ge(sub_ready, b.times(2, k + 1))

            def signal(ins, sm, s):
                ins.then_inc(sm, 1)
                dve.wait_ge(sm, s.times(1, 1))

            def step(s):
                a, b, c = s, s - 1, s - 2
                lb = Chain(dve_b, b, NBS)
                lc = Chain(dve_c, c, NC)
                if has_a(s):
                    if not s.first(2):
                        dve.wait_ge(xt_done, a.times(1, -1))
                    t = bass.ds(a.times(1), 1)
                    signal(dve.tensor_scalar(XN[:, a.odd, :], XA[:, t, :].rearrange("p t d -> p (t d)"),
                                             mv2[:, t, 0:1].rearrange("p t o -> p (t o)"), rstd2[:, t],
                                             ALU.subtract, ALU.mult), xn_ready, a)
                if has_b(s):
                    softmax_half(lb, b, 0)
                if has_c(s):
                    xr = XR[:, c.odd, :]
                    dve.wait_ge(wo_done, c.times(1, 1))
                    dve.wait_ge(res_ready, 4)
                    x1 = X1[:, bass.ds(c.times(1), 1), :].rearrange("p t d -> p (t d)")
                    dve.tensor_tensor(x1, WO_ps, x1, ALU.add).then_inc(x1_ready, 1)
                    hold(dve, x1_ready, c.times(1, 1))
                    if not c.first(2):
                        hold(dve, row_stored[c.odd], 16 * (c.off // 2) if c.i is None else c.i * 16 + 16 * (c.off // 2))
                    signal(layernorm(lc, xr[:, 0:D], x1), x2_ready, c)
                if has_b(s):
                    softmax_half(lb, b, 1)
                if has_c(s):
                    dve.wait_ge(gate_done, c.times(1, 1))
                    signal(dve.tensor_reduce(gmax[:, :], gate_ps, AX.X, ALU.max, negate=True), gmax_ready, c)
                    dve.wait_ge(gexp_ready, c.times(1, 1))
                    lc(dve.reciprocal(ginv[:, :], gsum[:, :]))
                    lc(dve.tensor_scalar(gexp[:, :], gexp[:, :], ginv[:, 0:1], None, ALU.mult), held=True)
                    lc(dve.max(top[:, :], gexp[:, :]), held=True)
                    lc(dve.max_index(topi[:, :], top[:, :], gexp[:, :]))
                    idx, wts, rws = (xr[:, META + k * TOPK:META + (k + 1) * TOPK] for k in range(3))
                    lc(dve.tensor_copy(idx, topi[:, 0:TOPK]))
                    lc(dve.tensor_reduce(wsum[:, :], top[:, 0:TOPK], AX.X, ALU.add))
                    lc(dve.tensor_scalar(wsum[:, :], wsum[:, :], 1e-20, None, ALU.add))
                    lc(dve.reciprocal(winv[:, :], wsum[:, :]))
                    lc(dve.tensor_scalar(wts, top[:, 0:TOPK], winv[:, 0:1], None, ALU.mult))
                    rr = result_row[:, bass.ds(c.times(1), 1), :].rearrange("p t k -> p (t k)")
                    signal(dve.tensor_copy(rws, rr), row_ready, c)
                    lc(dve.tensor_tensor(hot[:, :, :], iota_e[:, :].unsqueeze(1).broadcast_to([P, TOPK, EX]),
                                         idx.unsqueeze(2).broadcast_to([P, TOPK, EX]), ALU.is_equal))
                    signal(dve.tensor_reduce(M[:, :], hot[:, :, :].rearrange("p k e -> p e k"), AX.X, ALU.add),
                           m_ready, c)
                if has_b(s):
                    dve.wait_ge(pv_done, b.times(RG, RG))
                    if not b.first(2):
                        dve.wait_ge(aot_done, b.times(1, -1))
                    lb(dve.reciprocal(rden[:, :], O_ps[:, :, HD]))
                    signal(dve.tensor_tensor(AO[:, b.odd, :].rearrange("p (h v) -> p h v", h=H), O_ps[:, :, 0:HD],
                                             rden[:, :].unsqueeze(2).broadcast_to([P, H, HD]), ALU.mult), ao_ready, b)
                    lb.end()
                if has_c(s):
                    dve.wait_ge(pos_done, c.times(1, 1))
                    lc(dve.tensor_tensor(hotp[:, :, :], hot[:, :, :],
                                         pos_ps.unsqueeze(1).broadcast_to([P, TOPK, EX]), ALU.mult))
                    lc(dve.tensor_reduce(pos[:, :], hotp[:, :, :], AX.X, ALU.add))
                    lc(dve.tensor_tensor(Macc[:, :], Macc[:, :], M[:, :], ALU.add))
                    lc(dve.tensor_scalar(over[:, :], pos[:, :], float(CAP), float(BIG), ALU.is_ge, ALU.mult))
                    lc(dve.scalar_tensor_tensor(out=slotf[:, :], in0=idx, scalar=float(CAP), in1=pos[:, :],
                                                op0=ALU.mult, op1=ALU.add))
                    if not c.first(2):
                        dve.wait_ge(slot_stored[c.odd], (c.i * 96 if c.i is not None else 0) + 96 * (c.off // 2))
                    dve.tensor_copy(tid[:, c.odd:c.odd + 1], token_id[:, bass.ds(c.times(1), 1)])
                    signal(dve.tensor_tensor(slot[:, c.odd, :], slotf[:, :], over[:, :], ALU.add), slot_ready, c)
                    lc.end()

            steps(dve, step)
            dve.wait_ge(cnt_done, 1)
            dve.tensor_reduce(cmaxf[:, :], cnt_ps, AX.X, ALU.max).then_inc(dconst, 1)
            dve.wait_ge(dconst, 3)
            dve.tensor_copy(cmax[:, :], cmaxf[:, :]).then_inc(cmax_ready, 1)

            def shared(g):
                for f in range(3):
                    fw = min(P, FS - f * P)
                    dve.wait_ge(sh_silu, g.times(3, f + 1))
                    if not g.first() and f == 0:
                        dve.wait_ge(shd_done, g.times(SG // P))
                    dve.tensor_tensor(SH[0:fw, f, :], SS[0:fw, f % 2, :], PS[0:fw, 2 * (f % 2) + 1, :],
                                      ALU.mult).then_inc(sh_mul, 1)
                for t in range(SG // P):
                    dve.wait_ge(shd_done, g.times(SG // P, t + 1))
                    x1 = X1[:, bass.ds(g.times(SG // P, t), 1), :].rearrange("p t d -> p (t d)")
                    dve.tensor_tensor(x1, PS[:, 4 + t % 2, 0:D], x1, ALU.add).then_inc(sh_add, 1)

            shared(Step(0))
            with dve.Fori(0, T // SG - 1) as i:
                shared(Step(1, i, 1))

            dve.wait_ge(tab_loaded, 16)
            dve.tensor_copy(tabf[:, :, :], tabi[:, :, :]).then_inc(tab_f, 1)
            dve.wait_ge(tab_t, 1)
            dve.tensor_copy(tabT[:, :, :].rearrange("p e t -> p (e t)"), PS[:, 6, 0:2 * NTAB]).then_inc(tab_ready, 1)
            dve.wait_ge(tab_ready, 1)
            dve.wait_ge(sh_add, NT)
            most = dve.value_load(cmax[0:1, 0:1], min_val=0, max_val=T)

            def experts(base, nt, first):
                n = nt * P
                with dve.Fori(0, EX // UN) as i:
                    for j in range(UN):
                        e = Step(j, i, UN)
                        q = j % 2
                        link = Chain(dve_e, e, NE, base * NE)
                        dve.wait_ge(xg_loaded[j], i * (16 * nt) + (16 * nt + base // UN * 32))
                        dve.wait_ge(y_stored[j], i * (16 * nt) + base // UN * 32)
                        meta = XG[:, j, 0:nt, META:META + 3 * TOPK]
                        hh = hit[:, 0:nt, :]
                        link(dve.tensor_scalar(hh, meta[:, :, 0:TOPK], iota_e[:, bass.ds(e.times(1), 1)], None, ALU.is_equal))
                        link(dve.tensor_tensor(hitw[:, 0:nt, :], hh, meta[:, :, TOPK:2 * TOPK], ALU.mult))
                        link(dve.tensor_tensor(hitr[:, 0:nt, :], hh, meta[:, :, 2 * TOPK:3 * TOPK], ALU.mult))
                        link(dve.tensor_reduce(rsel[:, 0:nt], hitr[:, 0:nt, :], AX.X, ALU.add))
                        link(dve.tensor_reduce(wsel[:, j, 0:nt], hitw[:, 0:nt, :], AX.X, ALU.add))
                        dve.tensor_scalar(dest[:, j, 0:nt], rsel[:, 0:nt], float(BIG), None, ALU.add).then_inc(idx_ready, 1)
                        link.end()
                        dve.wait_ge(et_done, e.times(1, base + 1))
                        dve.wait_ge(gt_done, before(e, base, 1))
                        dve.tensor_copy(XET[:, q, :, 0:n], PS[:, q, :].rearrange("p (c n) -> p c n", c=DC)[:, :, 0:n])\
                           .then_inc(et_evac, 1)
                        dve.wait_ge(silu_ready, i * (2 * UN) + 2 * (base + j) + 1)
                        dve.wait_ge(dn_done, before(e, base, 1))
                        dve.tensor_tensor(HE[:, q, 0, 0:n], SL[:, q, 0, 0:n], PS[:, 2 + q, MAIN:MAIN + n], ALU.mult)\
                           .then_inc(h_ready, 1)
                        dve.wait_ge(silu_ready, i * (2 * UN) + 2 * (base + j) + 2)
                        dve.tensor_tensor(HE[0:FT, q, 1, 0:n], SL[0:FT, q, 1, 0:n], PS[64:64 + FT, 4, 0:n], ALU.mult)\
                           .then_inc(h_ready, 1)

            experts(0, MAIN // P, 0)
            with dve.If(most > MAIN):
                experts(EX, TPE - MAIN // P, MAIN // P)
                dve.wait_ge(tab_ready, 1)
            with dve.Else():
                dve.wait_ge(tab_ready, 1)

            def total(s):
                lo = 16 * (s.off // 2) + 16
                dve.wait_ge(yt_loaded[s.odd], s.i * 16 + lo)
                dve.wait_ge(out_stored[s.odd], s.i * 16)
                dve.tensor_reduce(YS[:, s.odd, :], YT[:, s.odd].rearrange("p k d -> p d k"), AX.X, ALU.add).then_inc(ysum, 1)
                dve.wait_ge(ysum, s.times(1, 1))
                x1 = X1[:, bass.ds(s.times(1), 1), :].rearrange("p t d -> p (t d)")
                dve.tensor_tensor(OUT[:, s.odd, :], YS[:, s.odd, :], x1, ALU.add).then_inc(out_ready, 1)

            with dve.Fori(0, NT // 2) as i:
                total(Step(0, i, 2))
                total(Step(1, i, 2))

        @block.gpsimd
        def _(pool):
            count = [0]

            def link(ins):
                count[0] += 1
                ins.then_inc(cst, 1)
                pool.wait_ge(cst, count[0])

            link(pool.memset(ident[:, :], 0.0))
            link(pool.affine_select(out=ident[:, :], in_=ident[:, :], compare_op=ALU.not_equal, fill=1.0, base=0,
                                    pattern=[[-1, P]], channel_multiplier=1))
            link(pool.memset(tri[:, :], 1.0))
            link(pool.affine_select(out=tri[:, :], in_=tri[:, :], compare_op=ALU.is_gt, fill=0.0, base=0,
                                    pattern=[[1, P]], channel_multiplier=-1))
            link(pool.memset(mask[:, :, :], 0.0))
            for k in range(NB):
                for t in range(2):
                    mk = mask[k * BLK:(k + 1) * BLK, t, 0:WK]
                    link(pool.affine_select(out=mk, in_=mk, compare_op=ALU.is_gt, fill=NEG, base=0,
                                            pattern=[[1, WK]], channel_multiplier=-1))
                    link(pool.affine_select(out=mk, in_=mk, compare_op=ALU.is_ge, fill=NEG, base=WIN,
                                            pattern=[[-1, WK]], channel_multiplier=1))
            link(pool.memset(mask[0:BLK, 0, 0:WIN], NEG))
            link(pool.iota(token_id[:, :], pattern=[[P, NT]], base=0, channel_multiplier=1))
            link(pool.iota(iota_e[:, :], pattern=[[1, EX]], base=0, channel_multiplier=0,
                           allow_small_or_imprecise_dtypes=True))
            link(pool.iota(result_row[:, :, :], pattern=[[P * TOPK, NT], [1, TOPK]], base=-BIG,
                           channel_multiplier=TOPK, allow_small_or_imprecise_dtypes=True))
            link(pool.memset(init_i[:, :], T))
            link(pool.memset(zero[:, :], 0.0))
            pool.memset(init_row[:, :], -1.0).then_inc(init_done, 1)
            for q in range(4):
                n = NT // 4
                pool.wait_ge(xa_ready, n * (q + 1))
                pool.tensor_tensor(X1[:, q * n:(q + 1) * n, :], X1[:, q * n:(q + 1) * n, :], XA[:, q * n:(q + 1) * n, :],
                                   ALU.add).then_inc(res_ready, 1)

            def step(s):
                if has_c(s):
                    c = s - 2
                    hold(pool, slot_ready, c.times(1, 1))
                    for k in range(TOPK):
                        pool.indirect_dma_start(table, bass.IndirectOffsetOnAxis(ap=slot[:, c.odd, k:k + 1], axis=0),
                                                tid[:, c.odd:c.odd + 1], None, bounds_check=EX * CAP - 1,
                                                oob_is_err=False).then_inc(slot_stored[c.odd], 16)

            pool.wait_ge(table_init, 32)
            steps(pool, step)
            for t in range(2):
                pool.wait_ge(slot_stored[t], 96 * NT // 2)
                pool.wait_ge(row_stored[t], 16 * NT // 2)
            pool.sem_inc(routed, 1)
            pool.wait_ge(tab_ready, 1)
            pool.wait_ge(all_stored, 1)
            most = pool.value_load(cmax[0:1, 0:1], min_val=0, max_val=T)

            def load(e, j, nt, first):
                pool.tensor_copy(gidx[:, j, 0:nt], tabT[:, bass.ds(e, 1), first:first + nt].rearrange("p e t -> p (e t)"))\
                    .then_inc(idx_free, 1)

            def start(j, nt, value):
                hold(pool, idx_free, value)
                for t in range(nt):
                    pool.indirect_dma_start(XG[:, j, t, :], None, rows,
                                            bass.IndirectOffsetOnAxis(ap=gidx[:, j, t:t + 1], axis=0),
                                            bounds_check=T, oob_is_err=False).then_inc(xg_loaded[j], 16)

            def scatter(i, j, base, nt):
                hold(pool, y_ready, i * UN + (base + j + 1))
                hold(pool, idx_ready, i * UN + (base + j + 1))
                for t in range(nt):
                    pool.indirect_dma_start(results, bass.IndirectOffsetOnAxis(ap=dest[:, j, t:t + 1], axis=0),
                                            YE[:, j, t, :], None, bounds_check=T * TOPK - 1,
                                            oob_is_err=False).then_inc(y_stored[j], 16)

            def experts(base, nt, first):
                for j in range(UN - 1):
                    load(j, j, nt, first)
                    start(j, nt, base + j + 1)
                with pool.Fori(0, EX // UN - 1) as i:
                    for j in range(UN):
                        n = j + UN - 1
                        if not (base == 0 and j == 0):
                            hold(pool, et_done, i * UN + (base + j))
                            hold(pool, idx_ready, i * UN + (base + j))
                        else:
                            hold(pool, et_done, i * UN)
                            hold(pool, idx_ready, i * UN)
                        load(i * UN + n, n % UN, nt, first)
                        start(n % UN, nt, i * UN + (base + n + 1))
                        scatter(i, j, base, nt)
                last = EX - UN
                pool.wait_ge(et_done, base + last)
                pool.wait_ge(idx_ready, base + last)
                load(EX - 1, UN - 1, nt, first)
                start(UN - 1, nt, base + EX)
                for j in range(UN):
                    pool.wait_ge(y_ready, base + last + j + 1)
                    for t in range(nt):
                        pool.indirect_dma_start(results, bass.IndirectOffsetOnAxis(ap=dest[:, j, t:t + 1], axis=0),
                                                YE[:, j, t, :], None, bounds_check=T * TOPK - 1,
                                                oob_is_err=False).then_inc(y_stored[j], 16)

            n0 = MAIN // P
            experts(0, n0, 0)
            for j in range(UN):
                pool.wait_ge(y_stored[j], 16 * n0 * EX // UN)
            with pool.If(most > MAIN):
                n1 = TPE - n0
                experts(EX, n1, n0)
                for j in range(UN):
                    pool.wait_ge(y_stored[j], 16 * (n0 + n1) * EX // UN)
                pool.sem_inc(all_stored, 1)
            with pool.Else():
                pool.sem_inc(all_stored, 1)


def kernel(**inputs):
    import numpy as _np
    import concourse.bacc as _bacc
    from concourse import mybir as _mybir
    from concourse.bass_utils import run_bass_kernel_spmd as _run

    a = {k: _np.asarray(v) for k, v in inputs.items()}
    wg = a["L0_ffn_w_gate"].transpose(0, 2, 1)
    wu = a["L0_ffn_w_up"].transpose(0, 2, 1)
    w1 = _np.zeros((EX, D, W1C), wg.dtype)
    w1[:, :, 0:P] = wg[:, :, 0:P]
    w1[:, :, P:2 * P] = wu[:, :, 0:P]
    w1[:, :, 2 * P:2 * P + FT] = wg[:, :, P:F]
    w1[:, :, 2 * P + 64:W1C] = wu[:, :, P:F]
    data = [
        ("x", a["L0_attn_x"].reshape(T, D)), ("glob", a["L0_attn_global_tokens"].reshape(G, D).T),
        ("ln_s", a["L0_attn_ln_scale"].reshape(DC, P).T), ("ln_b", a["L0_attn_ln_bias"].reshape(DC, P).T),
        ("wq", a["L0_attn_Wq"].T), ("wk", a["L0_attn_Wk"].T), ("wv", a["L0_attn_Wv"].T), ("wo", a["L0_attn_Wo"].T),
        ("gate", a["L0_ffn_gate_w"].T),
        ("w1", w1.reshape(EX, DC, P, W1C).transpose(0, 2, 1, 3)),
        ("w2", a["L0_ffn_w_down"].transpose(0, 2, 1)),
        ("shg", a["L0_ffn_sh_gate"].T), ("shu", a["L0_ffn_sh_up"].T), ("shd", a["L0_ffn_sh_down"].T),
    ]
    nc = _bacc.Bacc("TRN2", target_bir_lowering=False, num_devices=1)
    arrays, args = {}, []
    for name, v in data:
        v = _np.ascontiguousarray(v)
        arrays[f"in_{name}"] = v
        args.append(nc.dram_tensor(f"in_{name}", v.shape, _mybir.dt.from_np(v.dtype), kind="ExternalInput").ap())
    args.append(nc.dram_tensor("out", (T, D), F32, kind="ExternalOutput").ap())
    build(nc, *args)
    r = _run(nc, [arrays], core_ids=[0])
    return r.results[0]["out"].reshape(1, T, D)
```

```python
from contextlib import ExitStack

import concourse.bass as bass
from concourse import mybir

F32 = mybir.dt.float32
BF16 = mybir.dt.bfloat16
I32 = mybir.dt.int32
U32 = mybir.dt.uint32
ALU = mybir.AluOpType
ACT = mybir.ActivationFunctionType
AX = mybir.AxisListType

P = 128
T, D = 2048, 256
NT = T // P
DC = D // P
H, HD, G, WIN = 16, 16, 16, 32
BLK = 64
NB = P // BLK
WK = WIN + BLK
NK = WK + G
RG = 4
NJ = H // RG
HV = HD + 1
EX, TOPK, F, FS = 64, 6, 176, 352
CAP = 2 * ((T * TOPK + EX - 1) // EX)
MAIN = 256
TPE = CAP // P
FT = F - P
W1C = 2 * P + 64 + FT
META = D
ROW = 280
LN_EPS = 1e-5
SM_SCALE = float(HD) ** -0.5
NEG = -1e30
BIG = 1 << 15
UN = 4
SG = 512


class Step:

    def __init__(self, off, i=None, coef=0):
        self.off, self.i, self.coef = off, i, coef

    def __add__(self, n):
        return Step(self.off + n, self.i, self.coef)

    def __sub__(self, n):
        return self + -n

    def times(self, per, n=0):
        const = per * self.off + n
        return const if self.i is None else self.i * (per * self.coef) + const

    def turn(self, per, n=0, ring=UN):
        const = per * (self.off // ring) + n
        return const if self.i is None else self.i * (per * self.coef // ring) + const

    @property
    def slot(self):
        return self.off % UN

    @property
    def odd(self):
        return self.off % 2

    def first(self, n=1):
        return self.i is None and self.off < n


def build(nc, x, glob, ln_s, ln_b, wq, wk, wv, wo, gate, w1, w2, shg, shu, shd, out):
    table = nc.dram_tensor("slot_table", (EX * CAP, 1), I32, kind="Internal").ap()
    rows = nc.dram_tensor("token_rows", (T + 1, ROW), F32, kind="Internal").ap()
    results = nc.dram_tensor("results", (T * TOPK, D), F32, kind="Internal").ap()

    with ExitStack() as ctx:
        def sb(name, shape, dt=F32):
            return ctx.enter_context(nc.sbuf_tensor(name, shape, dt))

        def sem(name):
            return ctx.enter_context(nc.semaphore(name))

        def sem2(name, n=2):
            return [sem(f"{name}{j}") for j in range(n)]

        PS = ctx.enter_context(nc.psum_tensor("PS", [P, 8, 512], F32))

        passed = sem("passed")

        def hold(e, sm, value):
            e.wait_ge(sm, value)
            if not isinstance(value, int):
                e.sem_inc(passed, 1)

        ident = sb("ident", [P, P])
        tri = sb("tri", [P, P], BF16)
        ones = sb("ones", [P, P], BF16)
        mask = sb("mask", [P, 2, NB, NK])
        parity = sb("parity", [P, 2])
        iota_e = sb("iota_e", [P, EX])
        result_row = sb("result_row", [P, NT, TOPK])
        token_id = sb("token_id", [P, NT], I32)
        lns = sb("lns", [P, 2, DC])
        gT = sb("gT", [P, DC, G])
        wq_s, wk_s, wv_s, wo_s = (sb(n, [P, DC, D]) for n in ("wq_s", "wk_s", "wv_s", "wo_s"))
        gate_s = sb("gate_s", [P, DC, EX])
        shg_s = sb("shg_s", [P, DC, FS])
        shu_s = sb("shu_s", [P, DC, FS])
        shd_s = sb("shd_s", [P, 3, D])
        init_i = sb("init_i", [P, EX * CAP // P], I32)
        init_row = sb("init_row", [1, ROW])

        XA = sb("XA", [P, NT, D])
        XN = sb("XN", [P, 2, D])
        stats = sb("stats", [P, NT, 6])
        mv1 = sb("mv1", [P, NT, 2])
        mv2 = sb("mv2", [P, NT, 2])
        rstd1 = sb("rstd1", [P, NT])
        rstd2 = sb("rstd2", [P, NT])
        nmean2 = sb("nmean2", [P, NT])
        nv = sb("nv", [P, NT])
        ni = sb("ni", [P, NT], I32)
        ny = sb("ny", [P, NT])
        nt_ = sb("nt_", [P, NT])
        stats3 = sb("stats3", [P, 6])
        mv3 = sb("mv3", [P, 2])
        rstd3 = sb("rstd3", [P, 1])
        xnT = sb("xnT", [P, 2, DC, P])
        QT = sb("QT", [P, 2, DC, NB, 2, BLK])
        KW = sb("KW", [P, 2, DC, NB, NK])
        VS = sb("VS", [P, 2, H, HV])
        VW = sb("VW", [P, 2, NB, H, HV])
        SM = sb("SM", [P, 2, H, NK])
        smax = sb("smax", [P, H])
        PT = sb("PT", [P, 2, NJ, P])
        rden = sb("rden", [P, H])
        AO = sb("AO", [P, 2, D])
        AOT = sb("AOT", [P, 2, DC, P])
        X1 = sb("X1", [P, NT, D])
        XR = sb("XR", [P, 2, ROW])
        X2T = sb("X2T", [P, 2, DC, P])
        X2all = sb("X2all", [P, DC, T])
        gmax = sb("gmax", [P, 1])
        gexp = sb("gexp", [P, EX])
        gsum = sb("gsum", [P, 1])
        ginv = sb("ginv", [P, 1])
        top = sb("top", [P, 8])
        topi = sb("topi", [P, 8], U32)
        wsum = sb("wsum", [P, 1])
        winv = sb("winv", [P, 1])
        hot = sb("hot", [P, TOPK, EX])
        hotp = sb("hotp", [P, TOPK, EX])
        M = sb("M", [P, EX], BF16)
        Macc = sb("Macc", [P, EX], BF16)
        place = sb("place", [P, EX])
        over = sb("over", [P, TOPK])
        slotf = sb("slotf", [P, 2, TOPK])
        slot = sb("slot", [P, 2, TOPK], I32)
        tid = sb("tid", [P, 2], I32)
        cmaxf = sb("cmaxf", [P, 1])
        cmax = sb("cmax", [P, 1], I32)
        SS = sb("SS", [P, 2, SG])
        SH = sb("SH", [P, 3, SG])
        NTAB = EX * TPE // 2
        tabi = sb("tabi", [NTAB, 2, P], I32)
        tabf = sb("tabf", [NTAB, 2, P])
        tabT = sb("tabT", [P, EX, TPE])
        gidx = sb("gidx", [P, UN, 2], I32)
        W1 = sb("W1", [P, UN, DC, W1C])
        W2 = sb("W2", [P, UN, 2, D])
        XG = sb("XG", [P, UN, 2, ROW])
        XET = sb("XET", [P, 2, DC, MAIN])
        hit = sb("hit", [P, 2, TOPK])
        hitw = sb("hitw", [P, 2, TOPK])
        hitr = sb("hitr", [P, 2, TOPK])
        wsel = sb("wsel", [P, UN, 2])
        rsel = sb("rsel", [P, 2])
        dest = sb("dest", [P, UN, 2], I32)
        SL = sb("SL", [P, 2, 2, MAIN])
        HE = sb("HE", [P, 2, 2, MAIN])
        YE = sb("YE", [P, UN, 2, D])
        YT = sb("YT", [P, UN, TOPK, D])
        OUT, YS = XA[:, 0:UN, :], XA[:, UN:UN + 2, :]
        zero = sb("zero", [P, 2 * D])

        w_loaded = sem("w_loaded")
        sh_loaded = sem("sh_loaded")
        init_done = sem("init_done")
        dconst = sem("dconst")
        table_init = sem("table_init")
        glob_done, glob_evac = sem("glob_done"), sem("glob_evac")
        x_loaded = sem2("x_loaded", 4)
        dve_0 = sem("dve_0")
        dve_b, dve_c, dve_d = sem("dve_b"), sem("dve_c"), sem("dve_d")
        pool_d = sem("pool_d")
        norm_ready = sem("norm_ready")
        stat1, stat2 = sem("stat1"), sem("stat2")
        xa_ready, xn_ready, res_ready = sem("xa_ready"), sem("xn_ready"), sem("res_ready")
        xt_done, xt_evac = sem("xt_done"), sem("xt_evac")
        qk_done, v_done = sem("qk_done"), sem("v_done")
        qk_evac, v_evac = sem("qk_evac"), sem("v_evac")
        vw_loaded = sem2("vw_loaded")
        s_done, s_read = sem("s_done"), sem("s_read")
        max_ready, exp_ready = sem("max_ready"), sem("exp_ready")
        pt_done, pt_evac, pv_done = sem("pt_done"), sem("pt_evac"), sem("pv_done")
        ao_ready = sem("ao_ready")
        aot_done, aot_evac = sem("aot_done"), sem("aot_evac")
        wo_done, x1_ready, x2_ready = sem("wo_done"), sem("x1_ready"), sem("x2_ready")
        x2t_evac = sem("x2t_evac")
        gate_done, gmax_ready, gexp_ready = sem("gate_done"), sem("gmax_ready"), sem("gexp_ready")
        row_ready, row_stored = sem("row_ready"), sem2("row_stored")
        m_ready, pos_done, pos_evac = sem("m_ready"), sem("pos_done"), sem("pos_evac")
        slot_ready, slot_stored = sem("slot_ready"), sem2("slot_stored")
        cnt_done, cmax_ready = sem("cnt_done"), sem("cmax_ready")
        routed = sem("routed")
        sh_done, sh_silu, sh_mul = sem("sh_done"), sem("sh_silu"), sem("sh_mul")
        shd_done, sh_add = sem("shd_done"), sem("sh_add")
        tab_loaded, tab_f, tab_t, tab_ready = sem("tab_loaded"), sem("tab_f"), sem("tab_t"), sem("tab_ready")
        zeroed = sem("zeroed")
        ew_loaded = sem2("ew_loaded", UN)
        idx_ready = sem("idx_ready")
        xg_loaded = sem2("xg_loaded", UN)
        dve_e = sem("dve_e")
        et_done, et_evac = sem("et_done"), sem("et_evac")
        gu_done, gt_done = sem("gu_done"), sem("gt_done")
        silu_ready, h_ready = sem("silu_ready"), sem("h_ready")
        dn_done, y_ready = sem("dn_done"), sem("y_ready")
        y_stored = sem2("y_stored", UN)
        all_stored = sem("all_stored")
        yt_loaded = sem2("yt_loaded", UN)
        cst, idx_free = sem("cst"), sem("idx_free")
        ysum, out_ready = sem("ysum"), sem("out_ready")
        out_stored = sem2("out_stored", UN)

        S_ps = PS[:, 0:4, 0:NJ * NK].rearrange("p g (j k) -> p g j k", j=NJ)
        SM_v = SM[:, :, :, :].rearrange("p t (g j) k -> p t g j k", g=RG)
        PT_ps = PS[0:NK, 0:4, :].rearrange("p g (j q) -> p g j q", j=NJ)
        AOT_ps = PS[:, 4, 0:D].rearrange("p (c q) -> p c q", c=DC)
        X2T_ps = PS[:, 4, D:2 * D].rearrange("p (c q) -> p c q", c=DC)
        XT_ps = PS[:, 5, 0:D].rearrange("p (c q) -> p c q", c=DC)
        V_ps = PS[:, 5, D:2 * D]
        O_ps = PS[:, 5, 0:H * HV].rearrange("p (h v) -> p h v", h=H)
        WO_ps = PS[:, 6, 0:D]
        gate_ps = PS[:, 6, D:D + EX]
        pos_ps = PS[:, 6, D + EX:D + 2 * EX]
        cnt_ps = PS[:, 6, D + 2 * EX:D + 3 * EX]
        Q_ps = PS[:, 7, 0:D].rearrange("p (c q) -> p c q", c=DC)
        K_ps = PS[:, 7, D:2 * D].rearrange("p (c q) -> p c q", c=DC)

        def steps(engine, step):
            for j in range(PEEL):
                step(Step(j))
            with engine.Fori(0, (NT - PEEL) // 2) as i:
                step(Step(PEEL, i, 2))
                step(Step(PEEL + 1, i, 2))
            for j in range(3):
                step(Step(NT + j))

        def in_flight(engine, step):
            for j in range(UN):
                step(Step(j))
            with engine.Fori(0, EX // UN - 2) as i:
                for j in range(UN):
                    step(Step(UN + j, i, UN))
            for j in range(UN):
                step(Step(EX - UN + j))

        def has(e):
            return e.i is not None or 0 <= e.off < EX

        def has_a(s):
            return s.i is not None or s.off < NT

        def has_b(s):
            return s.i is not None or 1 <= s.off <= NT

        def has_c(s):
            return s.i is not None or 2 <= s.off <= NT + 1

        def has_d(s):
            return s.i is not None or s.off >= 3

        TAIL = (4, 7)
        NP = 12
        NW = 8
        PEEL = 6

        NBS, NC, ND, NE = 3, 12, 11, 5

        ctx.enter_context(nc.allow_low_precision(reason="whole numbers up to 16"))
        block = ctx.enter_context(nc.Block())

        @block.sync
        def _(sp):
            for q in range(4):
                n = NT // 4
                sp.dma_start(X1[:, q * n:(q + 1) * n, :], x[q * n * P:(q + 1) * n * P, :].rearrange("(t p) d -> p t d", p=P))\
                  .then_inc(x_loaded[q], 16)
            chunk = "(c p) n -> p c n"
            sp.dma_start(lns[:, 0, :], ln_s).then_inc(w_loaded, 16)
            sp.dma_start(lns[:, 1, :], ln_b).then_inc(w_loaded, 16)
            for dst, src in ((wq_s, wq), (wk_s, wk), (wv_s, wv), (gT, glob), (wo_s, wo), (gate_s, gate)):
                sp.dma_start(dst[:, :, :], src.rearrange(chunk, p=P)).then_inc(w_loaded, 16)
            sp.dma_start(shg_s[:, :, :], shg.rearrange(chunk, p=P)).then_inc(sh_loaded, 16)
            sp.wait_ge(init_done, 1)
            sp.dma_start(table.rearrange("(p n) o -> p (n o)", p=P), init_i[:, :]).then_inc(table_init, 16)
            sp.dma_start(rows[T:T + 1, :], init_row[:, :]).then_inc(table_init, 16)

            def weights(e, j):
                sp.dma_start(W1[:, j], w1[bass.ds(e, 1)].rearrange("e p c n -> p (e c) n")).then_inc(ew_loaded[j], 16)
                sp.dma_start(W2[:, j, 0, :], w2[bass.ds(e, 1), 0:P].rearrange("e p n -> p (e n)")).then_inc(ew_loaded[j], 16)
                sp.dma_start(W2[0:FT, j, 1, :], w2[bass.ds(e, 1), P:F].rearrange("e p n -> p (e n)")).then_inc(ew_loaded[j], 16)

            for j in range(UN):
                weights(j, j)

            def step(s):
                if has_a(s):
                    hold(sp, v_evac, s.times(1, 1))
                    if not s.first(2):
                        hold(sp, pv_done, s.times(RG, -RG))
                    sp.dma_start(VW[WIN:WK, s.odd, 0], VS[0:BLK, s.odd]).then_inc(vw_loaded[s.odd], 16)
                    sp.dma_start(VW[0:WK, s.odd, 1], VS[BLK - WIN:P, s.odd]).then_inc(vw_loaded[s.odd], 16)
                    if not s.first():
                        sp.dma_start(VW[0:WIN, s.odd, 0], VS[P - WIN:P, 1 - s.odd]).then_inc(vw_loaded[s.odd], 16)
                if has_d(s):
                    d = s - 3
                    hold(sp, row_ready, d.times(1, 1))
                    sp.dma_start(rows[bass.ds(d.times(P), P), :], XR[:, d.odd, :]).then_inc(row_stored[d.odd], 16)

            steps(sp, step)

            sp.wait_ge(routed, 1)
            sp.dma_start(tabi[:, :, :], table.rearrange("(c r s) o -> r c (s o)", c=2, s=P)).then_inc(tab_loaded, 16)
            sp.wait_ge(cmax_ready, 1)
            most = sp.value_load(cmax[0:1, 0:1], min_val=0, max_val=T)
            with sp.If(most > CAP):
                n = 2 * D
                v = results.rearrange("(a p r) d -> a p (r d)", p=P, r=n // D)
                for a in range(v.shape[0]):
                    sp.dma_start(v[a], zero[:, :]).then_inc(zeroed, 16)
                sp.wait_ge(zeroed, 16 * v.shape[0])
                sp.sem_inc(all_stored, 1)
            with sp.Else():
                sp.sem_inc(all_stored, 1)

            with sp.Fori(0, EX // UN - 1) as i:
                for j in range(UN):
                    hold(sp, dn_done, i * UN + (j + 1))
                    weights(i * UN + (j + UN), j)
            with sp.If(most > MAIN):
                with sp.Fori(0, EX // UN) as i:
                    for j in range(UN):
                        hold(sp, dn_done, i * UN + (EX - UN + j + 1))
                        weights(i * UN + j, j)
                sp.wait_ge(ew_loaded[0], 48)
            with sp.Else():
                sp.wait_ge(ew_loaded[0], 48)

            sp.wait_ge(all_stored, 2)
            res_v = results.rearrange("(t k) d -> t (k d)", k=TOPK)

            def results_in(t):
                if not t.first(UN):
                    hold(sp, ysum, t.times(1, 1 - UN))
                sp.dma_start(YT[:, t.slot].rearrange("p k d -> p (k d)"),
                             res_v[bass.ds(t.times(P), P), :]).then_inc(yt_loaded[t.slot], 16)

            for j in range(UN):
                results_in(Step(j))
            with sp.Fori(0, NT // UN - 1) as i:
                for j in range(UN):
                    results_in(Step(UN + j, i, UN))

        @block.tensor
        def _(pe):
            pe.wait_ge(w_loaded, 16 * NW)
            pe.wait_ge(init_done, 1)
            for c in range(DC):
                for d in range(DC):
                    pe.matmul(PS[:, 6, c * G:(c + 1) * G], wk_s[:, d, c * P:(c + 1) * P], gT[:, d, :],
                              start=(d == 0), stop=(d == DC - 1))
            for d in range(DC):
                mm = pe.matmul(PS[WK:NK, 7, 0:D], gT[:, d, :], wv_s[:, d, :], start=(d == 0), stop=(d == DC - 1),
                               tile_position=(0, WK))
            mm.then_inc(glob_done, 1)

            def scores(b):
                pe.wait_ge(qk_evac, b.times(1, 1))
                if not b.first():
                    pe.wait_ge(pt_evac, b.times(RG))
                for half in range(2):
                    for c in range(DC):
                        for k in range(NB):
                            for g in (2 * half, 2 * half + 1):
                                r = slice(32 * g, 32 * g + 32)
                                mm = pe.matmul(S_ps[:, g, NB * c + k, :],
                                               QT[r, b.odd, c, k].rearrange("p e q -> p (e q)"),
                                               KW[r, b.odd, c, k, :], start=True, stop=True)
                    mm.then_inc(s_done, 1)

            def step(s):
                a, b, c, d = s, s - 1, s - 2, s - 3
                if has_b(s):
                    scores(b)
                if has_c(s):
                    pe.wait_ge(ao_ready, c.times(1, 1))
                    for k in range(DC):
                        mm = pe.transpose(AOT_ps[:, k, :], AO[:, c.odd, k * P:(k + 1) * P], ident[:, :])
                if has_d(s):
                    pe.wait_ge(x2_ready, d.times(1, 1))
                    for k in range(DC):
                        mm = pe.transpose(X2T_ps[:, k, :], XR[:, d.odd, k * P:(k + 1) * P], ident[:, :])
                if has_c(s) or has_d(s):
                    mm.then_inc(aot_done, 1)
                if has_a(s):
                    pe.wait_ge(xn_ready, a.times(1, 1))
                    if s.first():
                        pe.wait_ge(glob_evac, 1)
                    if not s.first():
                        pe.wait_ge(v_evac, a.times(1))
                    for k in range(DC):
                        mm = pe.transpose(XT_ps[:, k, :], XN[:, a.odd, k * P:(k + 1) * P], ident[:, :])
                    mm.then_inc(xt_done, 1)
                if has_c(s):
                    pe.wait_ge(aot_evac, c.times(1, 1))
                    if not c.first(2):
                        pe.wait_ge(slot_ready, c.times(1, -1))
                    for k in range(DC):
                        mm = pe.matmul(WO_ps, AOT[:, c.odd, k, :], wo_s[:, k, :], start=(k == 0), stop=(k == DC - 1))
                    mm.then_inc(wo_done, 1)
                if has_a(s):
                    pe.wait_ge(xt_evac, a.times(1, 1))
                    if not s.first():
                        pe.wait_ge(qk_evac, a.times(1))
                    for ps, w in ((Q_ps, wq_s), (K_ps, wk_s)):
                        for k in range(DC):
                            for m in range(DC):
                                mm = pe.matmul(ps[:, k, :], w[:, m, k * P:(k + 1) * P], xnT[:, a.odd, m, :],
                                               start=(m == 0), stop=(m == DC - 1))
                    mm.then_inc(qk_done, 1)
                    for m in range(DC):
                        mm = pe.matmul(V_ps, xnT[:, a.odd, m, :], wv_s[:, m, :], start=(m == 0), stop=(m == DC - 1))
                    mm.then_inc(v_done, 1)
                if has_d(s):
                    pe.wait_ge(x2t_evac, d.times(1, 1))
                    if has_c(s):
                        pe.wait_ge(x1_ready, c.times(1, 1))
                    else:
                        pe.wait_ge(slot_ready, d.times(1))
                    for k in range(DC):
                        mm = pe.matmul(gate_ps, X2T[:, d.odd, k, :], gate_s[:, k, :], start=(k == 0), stop=(k == DC - 1))
                    mm.then_inc(gate_done, 1)
                if has_b(s):
                    def transposes(n):
                        pe.wait_ge(exp_ready, b.times(RG, 1 + n))
                        for k in range(NJ):
                            mm = pe.transpose(PT_ps[:, n, k, :], SM[:, b.odd, NJ * n + k, :], ident[:, :])
                        mm.then_inc(pt_done, 1)

                    def values(n):
                        pe.wait_ge(pt_evac, b.times(RG, n + 1))
                        if n == 0:
                            lo = 48 * (b.off // 2) + 48 - (0 if b.odd else 16)
                            pe.wait_ge(vw_loaded[b.odd], lo if b.i is None else b.i * 48 + lo)
                            pe.wait_ge(v_evac, min(b.off + 2, NT) if b.i is None else b.times(1, 2))
                        for k in range(DC):
                            for e in range(2):
                                h = 8 * k + 2 * n + e
                                for q in range(NB):
                                    mm = pe.matmul(O_ps[q * BLK:(q + 1) * BLK, h, :],
                                                   PT[0:NK, n % 2, NB * k + q, e * BLK:(e + 1) * BLK],
                                                   VW[0:NK, b.odd, q, h, :], start=True, stop=True)
                        mm.then_inc(pv_done, 1)

                    for n in range(RG):
                        transposes(n)
                    for n in range(RG):
                        values(n)
                if has_d(s):
                    pe.wait_ge(m_ready, d.times(1, 1))
                    pe.wait_ge(gexp_ready, d.times(1, 1))
                    pe.matmul(pos_ps, tri[:, :], M[:, :], start=True, stop=False)
                    pe.matmul(pos_ps, ones[:, :], Macc[:, :], start=False, stop=True).then_inc(pos_done, 1)

            steps(pe, step)

            pe.wait_ge(slot_ready, NT)
            pe.matmul(cnt_ps, ones[:, :], Macc[:, :], start=True, stop=True).then_inc(cnt_done, 1)

            pe.wait_ge(sh_loaded, 16 * 4)

            def shared(g):
                for f in range(3):
                    fw = min(P, FS - f * P)
                    n = 3 * 1
                    if g.first() and f < 2:
                        pass
                    else:
                        pe.wait_ge(sh_mul, g.times(3, f - 1))
                    par = f % 2
                    for u, w in enumerate((shg_s, shu_s)):
                        for d in range(DC):
                            mm = pe.matmul(PS[0:fw, 2 * par + u, :], w[:, d, f * P:f * P + fw],
                                           X2all[:, d, bass.ds(g.times(SG), SG)], start=(d == 0), stop=(d == DC - 1))
                    mm.then_inc(sh_done, 1)
                pe.wait_ge(sh_mul, g.times(3, 3))
                for t in range(SG // P):
                    if not (g.first() and t < 2):
                        pe.wait_ge(sh_add, g.times(SG // P, t - 1))
                    for f in range(3):
                        fw = min(P, FS - f * P)
                        mm = pe.matmul(PS[:, 4 + t % 2, 0:D], SH[0:fw, f, t * P:(t + 1) * P], shd_s[0:fw, f, :],
                                       start=(f == 0), stop=(f == 2))
                    mm.then_inc(shd_done, 1)

            pe.wait_ge(cmax_ready, 1)
            shared(Step(0))
            pe.wait_ge(tab_f, 1)
            for k in range(2):
                mm = pe.transpose(PS[:, 6, k * NTAB:(k + 1) * NTAB], tabf[:, k, :], ident[0:NTAB, 0:NTAB])
            mm.then_inc(tab_t, 1)
            with pe.Fori(0, T // SG - 1) as i:
                shared(Step(1, i, 1))

            pe.wait_ge(tab_ready, 1)
            pe.wait_ge(sh_add, NT)
            most = pe.value_load(cmax[0:1, 0:1], min_val=0, max_val=T)

            def experts(base, nt):
                n = nt * P

                def rows_t(e):
                    pe.wait_ge(xg_loaded[e.slot], e.turn(16 * nt, 16 * nt + base * 32 // UN))
                    if base or not e.first(2):
                        pe.wait_ge(et_evac, e.times(1, base - 1))
                    for t in range(nt):
                        for d in range(DC):
                            mm = pe.transpose(PS[:, e.odd, d * MAIN + t * P:d * MAIN + (t + 1) * P],
                                              XG[:, e.slot, t, d * P:(d + 1) * P], ident[:, :])
                    mm.then_inc(et_done, 1)

                def hidden(e):
                    j, q = e.slot, e.odd
                    pe.wait_ge(ew_loaded[j], e.turn(48, 48 + base * 48 // UN))
                    pe.wait_ge(et_evac, e.times(1, base + 1))
                    if base or not e.first(2):
                        pe.wait_ge(h_ready, e.times(2, 2 * base - 2))
                    for u in range(2):
                        for d in range(DC):
                            mm = pe.matmul(PS[:, 2 + q, u * MAIN:u * MAIN + n], W1[:, j, d, u * P:(u + 1) * P],
                                           XET[:, q, d, 0:n], start=(d == 0), stop=(d == DC - 1))
                    mm.then_inc(gu_done, 1)
                    for d in range(DC):
                        mm = pe.matmul(PS[0:W1C - 2 * P, TAIL[q], 0:n], W1[:, j, d, 2 * P:W1C], XET[:, q, d, 0:n],
                                       start=(d == 0), stop=(d == DC - 1))
                    mm.then_inc(gt_done, 1)

                def down(e):
                    j, q = e.slot, e.odd
                    pe.wait_ge(h_ready, e.times(2, 2 * base + 2))
                    if base or not e.first(2):
                        pe.wait_ge(y_ready, e.times(1, base - 1))
                    for t in range(nt):
                        pe.matmul(PS[:, 5 + q, t * D:(t + 1) * D], HE[:, q, 0, t * P:(t + 1) * P], W2[:, j, 0, :],
                                  start=True, stop=False)
                        mm = pe.matmul(PS[:, 5 + q, t * D:(t + 1) * D], HE[0:FT, q, 1, t * P:(t + 1) * P],
                                       W2[0:FT, j, 1, :], start=False, stop=True)
                    mm.then_inc(dn_done, 1)

                def step(e):
                    if has(e + 1):
                        hidden(e + 1)
                    if has(e + 2):
                        rows_t(e + 2)
                    down(e)

                rows_t(Step(0))
                rows_t(Step(1))
                hidden(Step(0))
                in_flight(pe, step)

            experts(0, MAIN // P)
            with pe.If(most > MAIN):
                experts(EX, TPE - MAIN // P)
                pe.wait_ge(tab_ready, 1)
            with pe.Else():
                pe.wait_ge(tab_ready, 1)

        @block.scalar
        def _(act):
            act.dma_start(shu_s[:, :, :], shu.rearrange("(c p) n -> p c n", p=P)).then_inc(sh_loaded, 16)
            act.dma_start(shd_s[:, 0:2, :], shd[0:2 * P, :].rearrange("(c p) n -> p c n", p=P)).then_inc(sh_loaded, 16)
            act.dma_start(shd_s[0:FS - 2 * P, 2, :], shd[2 * P:FS, :]).then_inc(sh_loaded, 16)
            act.wait_ge(w_loaded, 16 * NW)
            act.wait_ge(dconst, 2)
            act.wait_ge(glob_done, 1)
            gk = PS[:, 6, 0:DC * G].rearrange("p (c g) -> p c g", c=DC)
            for t in range(2):
                for k in range(NB):
                    act.copy(KW[:, t, :, k, WK:NK], gk)
                    a = act.copy(VW[WK:NK, t, k, :, 0:HD], PS[WK:NK, 7, 0:D].rearrange("p (h v) -> p h v", h=H))
            a.then_inc(glob_evac, 1)

            def normalise(a):
                t = bass.ds(a.times(1), 1)
                if not a.first(2):
                    act.wait_ge(xt_done, a.times(1, -1))
                act.activation(XN[:, a.odd, :], XA[:, t, :].rearrange("p t d -> p (t d)"), ACT.Identity,
                               bias=nmean2[:, t], scale=rstd2[:, t]).then_inc(xn_ready, 1)

            def exps(b, g):
                act.wait_ge(max_ready, b.times(2, g // 2 + 1))
                for k in range(NJ):
                    h = NJ * g + k
                    i = act.activation(SM[:, b.odd, h], SM[:, b.odd, h], ACT.Exp, bias=smax[:, h:h + 1])
                i.then_inc(exp_ready, 1)

            def step(s):
                a, b, c, d = s, s - 1, s - 2, s - 3
                if has_a(s):
                    normalise(a)
                if has_b(s):
                    exps(b, 0)
                if has_c(s):
                    act.wait_ge(aot_done, c.times(1, 1))
                    act.copy(AOT[:, c.odd], AOT_ps).then_inc(aot_evac, 1)
                if has_d(s):
                    act.wait_ge(aot_done, d.times(1, 2))
                    act.copy(X2T[:, d.odd], X2T_ps)
                    act.copy(X2all[:, :, bass.ds(d.times(P), P)], X2T_ps).then_inc(x2t_evac, 1)
                if has_a(s):
                    act.wait_ge(xt_done, a.times(1, 1))
                    if not s.first(2):
                        act.wait_ge(v_done, a.times(1, -1))
                    for k in range(DC):
                        i = act.activation(xnT[:, a.odd, k, :], XT_ps[:, k, :], ACT.Identity,
                                           bias=lns[:, 1, k:k + 1], scale=lns[:, 0, k:k + 1])
                    i.then_inc(xt_evac, 1)
                if has_b(s):
                    exps(b, 1)
                    exps(b, 2)
                    exps(b, 3)
                if has_a(s):
                    act.wait_ge(qk_done, a.times(1, 1))
                    if not s.first(2):
                        act.wait_ge(s_done, a.times(2, -2))
                    for e in range(2):
                        act.mul(QT[:, a.odd, :, :, e, :], Q_ps.rearrange("p c (k q) -> p c k q", k=NB), parity[:, e:e + 1])
                    if s.first():
                        act.copy(KW[:, 0, :, 0, 0:WIN], KW[:, 1, :, 1, WK - WIN:WK])
                    else:
                        act.wait_ge(qk_evac, a.times(1))
                        act.copy(KW[:, a.odd, :, 0, 0:WIN], KW[:, 1 - a.odd, :, 1, WK - WIN:WK])
                    act.copy(KW[:, a.odd, :, 0, WIN:WK], K_ps[:, :, 0:BLK])
                    act.copy(KW[:, a.odd, :, 1, 0:WK], K_ps[:, :, BLK - WIN:P]).then_inc(qk_evac, 1)
                    act.wait_ge(v_done, a.times(1, 1))
                    if not s.first(2):
                        p = a - 1
                        lo = 48 * (p.off // 2) + 48 - (0 if p.odd else 16)
                        act.wait_ge(vw_loaded[p.odd], lo if p.i is None else p.i * 48 + lo)
                    act.copy(VS[:, a.odd, :, 0:HD], V_ps.rearrange("p (h v) -> p h v", h=H)).then_inc(v_evac, 1)

                def gate_exp():
                    act.wait_ge(gmax_ready, d.times(1, 1))
                    act.activation(gexp[:, :], gate_ps, ACT.Exp, bias=gmax[:, 0:1],
                                   accum_out=gsum[:, 0:1]).then_inc(gexp_ready, 1)

                if has_b(s):
                    for n in range(RG):
                        act.wait_ge(pt_done, b.times(RG, n + 1))
                        if not (b.first() and n < 2):
                            act.wait_ge(pv_done, b.times(RG, n - 1))
                        act.copy(PT[0:NK, n % 2], PT_ps[:, n]).then_inc(pt_evac, 1)
                        if n == 1 and has_d(s):
                            gate_exp()
                elif has_d(s):
                    gate_exp()
                if has_d(s):
                    act.wait_ge(pos_done, d.times(1, 1))
                    if not d.first():
                        act.wait_ge(slot_ready, d.times(1))
                    act.copy(place[:, :], pos_ps).then_inc(pos_evac, 1)

            act.wait_ge(norm_ready, 1)
            steps(act, step)

            def shared(g):
                for f in range(3):
                    fw = min(P, FS - f * P)
                    act.wait_ge(sh_done, g.times(3, f + 1))
                    if not (g.first() and f < 2):
                        act.wait_ge(sh_mul, g.times(3, f - 1))
                    act.activation(SS[0:fw, f % 2, :], PS[0:fw, 2 * (f % 2), :], ACT.Silu).then_inc(sh_silu, 1)

            shared(Step(0))
            with act.Fori(0, T // SG - 1) as i:
                shared(Step(1, i, 1))

            act.wait_ge(cmax_ready, 1)
            most = act.value_load(cmax[0:1, 0:1], min_val=0, max_val=T)

            def experts(base, nt):
                n = nt * P

                def silus(e):
                    q = e.odd
                    act.wait_ge(gu_done, e.times(1, base + 1))
                    if base or not e.first(2):
                        act.wait_ge(h_ready, e.times(2, 2 * base - 2))
                    act.activation(SL[:, q, 0, 0:n], PS[:, 2 + q, 0:n], ACT.Silu).then_inc(silu_ready, 1)
                    act.wait_ge(gt_done, e.times(1, base + 1))
                    act.activation(SL[0:FT, q, 1, 0:n], PS[0:FT, TAIL[q], 0:n], ACT.Silu).then_inc(silu_ready, 1)

                def weighted(e):
                    act.wait_ge(dn_done, e.times(1, base + 1))
                    act.wait_ge(idx_ready, e.times(1, base + 1))
                    if base or not e.first(UN):
                        act.wait_ge(y_stored[e.slot], e.turn(16 * nt, base // UN * 32))
                    for t in range(nt):
                        i = act.mul(YE[:, e.slot, t, :], PS[:, 5 + e.odd, t * D:(t + 1) * D], wsel[:, e.slot, t:t + 1])
                    i.then_inc(y_ready, 1)

                def step(e):
                    if has(e + 1):
                        silus(e + 1)
                    weighted(e)

                silus(Step(0))
                in_flight(act, step)

            experts(0, MAIN // P)
            with act.If(most > MAIN):
                experts(EX, TPE - MAIN // P)
                act.wait_ge(cmax_ready, 1)
            with act.Else():
                act.wait_ge(cmax_ready, 1)

            def store(t):
                act.wait_ge(out_ready, t.times(1, 1))
                act.dma_start(out[bass.ds(t.times(P), P), :], OUT[:, t.slot, :]).then_inc(out_stored[t.slot], 16)

            with act.Fori(0, NT // UN) as i:
                for j in range(UN):
                    store(Step(j, i, UN))
            for j in range(UN):
                act.wait_ge(out_stored[j], 16 * NT // UN)

        @block.vector
        def _(dve):
            dve.memset(VS[:, :, :, HD:HV], 1.0)
            dve.memset(VW[:, :, :, :, :], 1.0)
            dve.memset(KW[:, :, :, :, :], 0.0)
            dve.memset(Macc[:, :], 0.0)
            dve.memset(XR[:, :, :], 0.0)
            dve.memset(ones[:, :], 1.0).then_inc(dconst, 1)
            dve.wait_ge(init_done, 1)
            dve.tensor_reduce(parity[:, :], ident[:, :].rearrange("p (b e d) -> p e b d", e=2, d=HD), AX.XY, ALU.add)\
               .then_inc(dconst, 1)
            dve.wait_ge(dconst, 2)

            class Chain:

                def __init__(self, sem, s, per, base=0):
                    self.sem, self.s, self.per, self.n, self.base = sem, s, per, 0, base

                def __call__(self, ins, held=False):
                    self.n += 1
                    ins.then_inc(self.sem, 1)
                    value = self.s.times(self.per, self.base + self.n)
                    if held:
                        hold(dve, self.sem, value)
                    else:
                        dve.wait_ge(self.sem, value)

                def end(self):
                    assert self.n == self.per, (self.n, self.per)

            def rsqrt(link, dst, var, n):
                v, y, t, b = nv[:, 0:n], ny[:, 0:n], nt_[:, 0:n], ni[:, 0:n]
                link(dve.tensor_scalar(v, var, LN_EPS, None, ALU.add))
                link(dve.tensor_scalar(b, v.bitcast(I32), 1, None, ALU.logical_shift_right))
                link(dve.tensor_scalar(y.bitcast(I32), b, -1.0, float(0x5F3759DF), ALU.mult, ALU.add))
                link(dve.tensor_scalar(v, v, -0.5, None, ALU.mult))
                for k in range(3):
                    link(dve.tensor_tensor(t, y, y, ALU.mult))
                    link(dve.tensor_tensor(t, t, v, ALU.mult))
                    link(dve.scalar_tensor_tensor(out=dst if k == 2 else y, in0=t, scalar=1.5, in1=y,
                                                  op0=ALU.add, op1=ALU.mult))

            link0 = Chain(dve_0, Step(0), 0)
            for t in range(NT):
                if t % (NT // 4) == 0:
                    dve.wait_ge(x_loaded[t // (NT // 4)], 16)
                dve.bn_stats(stats[:, t, :], X1[:, t, :]).then_inc(stat1, 1)
            dve.wait_ge(stat1, NT)
            for t in range(NT):
                dve.bn_aggr(mv1[:, t, :], stats[:, t, :]).then_inc(stat1, 1)
            dve.wait_ge(stat1, 2 * NT)
            rsqrt(link0, rstd1[:, :], mv1[:, :, 1], NT)
            for t in range(NT):
                dve.tensor_scalar(XA[:, t, :], X1[:, t, :], mv1[:, t, 0:1], rstd1[:, t:t + 1], ALU.subtract, ALU.mult)\
                   .then_inc(xa_ready, 1)
            for t in range(NT):
                dve.wait_ge(xa_ready, t + 1)
                dve.bn_stats(stats[:, t, :], XA[:, t, :]).then_inc(stat2, 1)
            dve.wait_ge(stat2, NT)
            for t in range(NT):
                dve.bn_aggr(mv2[:, t, :], stats[:, t, :]).then_inc(stat2, 1)
            dve.wait_ge(stat2, 2 * NT)
            rsqrt(link0, rstd2[:, :], mv2[:, :, 1], NT)
            dve.scalar_tensor_tensor(out=nmean2[:, :], in0=mv2[:, :, 0], scalar=-1.0, in1=rstd2[:, :],
                                     op0=ALU.mult, op1=ALU.mult).then_inc(norm_ready, 1)

            def layernorm(link, dst, src):
                link(dve.bn_stats(stats3[:, :], src), held=True)
                link(dve.bn_aggr(mv3[:, :], stats3[:, :]))
                v, y, t, b = nv[:, 0:1], ny[:, 0:1], nt_[:, 0:1], ni[:, 0:1]
                link(dve.tensor_scalar(v, mv3[:, 1:2], LN_EPS, None, ALU.add))
                link(dve.tensor_scalar(b, v.bitcast(I32), 1, None, ALU.logical_shift_right))
                link(dve.tensor_scalar(y.bitcast(I32), b, -1.0, float(0x5F3759DF), ALU.mult, ALU.add))
                link(dve.tensor_scalar(v, v, -0.5, None, ALU.mult))
                for k in range(3):
                    link(dve.scalar_tensor_tensor(out=t, in0=y, scalar=v, in1=y, op0=ALU.mult, op1=ALU.mult))
                    link(dve.scalar_tensor_tensor(out=rstd3[:, :] if k == 2 else y, in0=t, scalar=1.5, in1=y,
                                                  op0=ALU.add, op1=ALU.mult))
                return dve.tensor_scalar(dst, src, mv3[:, 0:1], rstd3[:, 0:1], ALU.subtract, ALU.mult)

            def split(v):
                return v.rearrange("p (c k) n -> p c k n", c=DC)

            def softmax_half(link, b, k):
                mk = mask[:, 0 if b.first() else 1]
                dve.wait_ge(s_done, b.times(2, k + 1))
                if k == 0 and not b.first(2):
                    dve.wait_ge(pt_done, b.times(RG, -RG))
                for gg in range(2):
                    i = dve.scalar_tensor_tensor(out=split(SM_v[:, b.odd, 2 * k + gg]), in0=split(S_ps[:, 2 * k + gg]),
                                                 scalar=SM_SCALE, in1=mk.unsqueeze(1).broadcast_to([P, DC, NB, NK]),
                                                 op0=ALU.mult, op1=ALU.add)
                    if gg:
                        i.then_inc(s_read, 1)
                    else:
                        link(i)
                dve.wait_ge(s_read, b.times(2, k + 1))
                if k == 0 and not b.first():
                    dve.wait_ge(exp_ready, b.times(RG))
                h = slice(8 * k, 8 * k + 8)
                dve.tensor_reduce(smax[:, h], SM[:, b.odd, h, :], AX.X, ALU.max, negate=True).then_inc(max_ready, 1)

            def signal(ins, sm, s):
                ins.then_inc(sm, 1)
                dve.wait_ge(sm, s.times(1, 1))

            def step(s):
                b, c, d = s - 1, s - 2, s - 3
                lb = Chain(dve_b, b, NBS)
                lc = Chain(dve_c, c, NC)
                ld = Chain(dve_d, d, ND)
                if has_b(s):
                    softmax_half(lb, b, 0)
                    softmax_half(lb, b, 1)
                if has_c(s):
                    xr = XR[:, c.odd, :]
                    dve.wait_ge(wo_done, c.times(1, 1))
                    dve.wait_ge(res_ready, 4)
                    x1 = X1[:, bass.ds(c.times(1), 1), :].rearrange("p t d -> p (t d)")
                    dve.tensor_tensor(x1, WO_ps, x1, ALU.add).then_inc(x1_ready, 1)
                    hold(dve, x1_ready, c.times(1, 1))
                    if not c.first(2):
                        hold(dve, row_stored[c.odd], c.turn(16, ring=2))
                    signal(layernorm(lc, xr[:, 0:D], x1), x2_ready, c)
                    lc.end()
                if has_d(s):
                    xr = XR[:, d.odd, :]
                    dve.wait_ge(gate_done, d.times(1, 1))
                    signal(dve.tensor_reduce(gmax[:, :], gate_ps, AX.X, ALU.max, negate=True), gmax_ready, d)
                    dve.wait_ge(gexp_ready, d.times(1, 1))
                    ld(dve.reciprocal(ginv[:, :], gsum[:, :]))
                    ld(dve.tensor_scalar(gexp[:, :], gexp[:, :], ginv[:, 0:1], None, ALU.mult), held=True)
                    ld(dve.max(top[:, :], gexp[:, :]), held=True)
                    ld(dve.max_index(topi[:, :], top[:, :], gexp[:, :]))
                    idx, wts, rws = (xr[:, META + k * TOPK:META + (k + 1) * TOPK] for k in range(3))
                    ld(dve.tensor_copy(idx, topi[:, 0:TOPK]))
                    if not d.first():
                        dve.wait_ge(slot_ready, d.times(1))
                    ld(dve.tensor_scalar(slotf[:, d.odd, :], idx, float(CAP), -float(BIG * (CAP - 1)), ALU.mult, ALU.add))
                    ld(dve.tensor_tensor(hot[:, :, :], iota_e[:, :].unsqueeze(1).broadcast_to([P, TOPK, EX]),
                                         idx.unsqueeze(2).broadcast_to([P, TOPK, EX]), ALU.is_equal))
                    signal(dve.tensor_reduce(M[:, :], hot[:, :, :].rearrange("p k e -> p e k"), AX.X, ALU.add),
                           m_ready, d)
                    ld(dve.tensor_reduce(wsum[:, :], top[:, 0:TOPK], AX.X, ALU.add))
                    ld(dve.tensor_scalar(wsum[:, :], wsum[:, :], 1e-20, None, ALU.add))
                    ld(dve.reciprocal(winv[:, :], wsum[:, :]))
                    ld(dve.tensor_scalar(wts, top[:, 0:TOPK], winv[:, 0:1], None, ALU.mult))
                    rr = result_row[:, bass.ds(d.times(1), 1), :].rearrange("p t k -> p (t k)")
                    signal(dve.tensor_copy(rws, rr), row_ready, d)
                if has_b(s):
                    dve.wait_ge(pv_done, b.times(RG, RG))
                    if not b.first(2):
                        dve.wait_ge(aot_done, b.times(1, -1))
                    lb(dve.reciprocal(rden[:, :], O_ps[:, :, HD]))
                    signal(dve.tensor_tensor(AO[:, b.odd, :].rearrange("p (h v) -> p h v", h=H), O_ps[:, :, 0:HD],
                                             rden[:, :].unsqueeze(2).broadcast_to([P, H, HD]), ALU.mult), ao_ready, b)
                    lb.end()
                if has_d(s):
                    ld.end()

            steps(dve, step)
            dve.wait_ge(cnt_done, 1)
            dve.tensor_reduce(cmaxf[:, :], cnt_ps, AX.X, ALU.max).then_inc(dconst, 1)
            dve.wait_ge(dconst, 3)
            dve.tensor_copy(cmax[:, :], cmaxf[:, :]).then_inc(cmax_ready, 1)

            def shared(g):
                for f in range(3):
                    fw = min(P, FS - f * P)
                    dve.wait_ge(sh_silu, g.times(3, f + 1))
                    if not g.first() and f == 0:
                        dve.wait_ge(shd_done, g.times(SG // P))
                    dve.tensor_tensor(SH[0:fw, f, :], SS[0:fw, f % 2, :], PS[0:fw, 2 * (f % 2) + 1, :],
                                      ALU.mult).then_inc(sh_mul, 1)
                for t in range(SG // P):
                    dve.wait_ge(shd_done, g.times(SG // P, t + 1))
                    x1 = X1[:, bass.ds(g.times(SG // P, t), 1), :].rearrange("p t d -> p (t d)")
                    dve.tensor_tensor(x1, PS[:, 4 + t % 2, 0:D], x1, ALU.add).then_inc(sh_add, 1)

            shared(Step(0))
            dve.wait_ge(tab_loaded, 16)
            dve.tensor_copy(tabf[:, :, :], tabi[:, :, :]).then_inc(tab_f, 1)
            dve.wait_ge(tab_t, 1)
            dve.tensor_copy(tabT[:, :, :].rearrange("p e t -> p (e t)"), PS[:, 6, 0:2 * NTAB]).then_inc(tab_ready, 1)
            with dve.Fori(0, T // SG - 1) as i:
                shared(Step(1, i, 1))

            dve.wait_ge(tab_ready, 1)
            dve.wait_ge(sh_add, NT)
            most = dve.value_load(cmax[0:1, 0:1], min_val=0, max_val=T)

            def experts(base, nt):
                n = nt * P

                def choices(e):
                    j = e.slot
                    link = Chain(dve_e, e, NE, base * NE)
                    dve.wait_ge(xg_loaded[j], e.turn(16 * nt, 16 * nt + base // UN * 32))
                    if base or not e.first(UN):
                        dve.wait_ge(y_stored[j], e.turn(16 * nt, base // UN * 32))
                    meta = XG[:, j, 0:nt, META:META + 3 * TOPK]
                    hh = hit[:, 0:nt, :]
                    link(dve.tensor_scalar(hh, meta[:, :, 0:TOPK], iota_e[:, bass.ds(e.times(1), 1)], None, ALU.is_equal))
                    link(dve.tensor_tensor(hitw[:, 0:nt, :], hh, meta[:, :, TOPK:2 * TOPK], ALU.mult))
                    link(dve.tensor_tensor(hitr[:, 0:nt, :], hh, meta[:, :, 2 * TOPK:3 * TOPK], ALU.mult))
                    link(dve.tensor_reduce(rsel[:, 0:nt], hitr[:, 0:nt, :], AX.X, ALU.add))
                    link(dve.tensor_reduce(wsel[:, j, 0:nt], hitw[:, 0:nt, :], AX.X, ALU.add))
                    dve.tensor_scalar(dest[:, j, 0:nt], rsel[:, 0:nt], float(BIG), None, ALU.add).then_inc(idx_ready, 1)
                    link.end()

                def rows_t(e):
                    dve.wait_ge(et_done, e.times(1, base + 1))
                    if base or not e.first(2):
                        dve.wait_ge(gt_done, e.times(1, base - 1))
                    dve.tensor_copy(XET[:, e.odd, :, 0:n],
                                    PS[:, e.odd, :].rearrange("p (c n) -> p c n", c=DC)[:, :, 0:n]).then_inc(et_evac, 1)

                def products(e):
                    q = e.odd
                    dve.wait_ge(silu_ready, e.times(2, 2 * base + 1))
                    if base or not e.first(2):
                        dve.wait_ge(dn_done, e.times(1, base - 1))
                    dve.tensor_tensor(HE[:, q, 0, 0:n], SL[:, q, 0, 0:n], PS[:, 2 + q, MAIN:MAIN + n], ALU.mult)\
                       .then_inc(h_ready, 1)
                    dve.wait_ge(silu_ready, e.times(2, 2 * base + 2))
                    dve.tensor_tensor(HE[0:FT, q, 1, 0:n], SL[0:FT, q, 1, 0:n], PS[64:64 + FT, TAIL[q], 0:n], ALU.mult)\
                       .then_inc(h_ready, 1)

                def step(e):
                    if has(e + 1):
                        products(e + 1)
                    if has(e + 2):
                        rows_t(e + 2)
                    if has(e + 1):
                        choices(e + 1)

                rows_t(Step(0))
                rows_t(Step(1))
                choices(Step(0))
                products(Step(0))
                in_flight(dve, step)

            experts(0, MAIN // P)
            with dve.If(most > MAIN):
                experts(EX, TPE - MAIN // P)
                dve.wait_ge(tab_ready, 1)
            with dve.Else():
                dve.wait_ge(tab_ready, 1)

            dve.wait_ge(xn_ready, NT)
            dve.wait_ge(res_ready, 4)

            def total(t):
                dve.wait_ge(yt_loaded[t.slot], t.turn(16, 16))
                if not t.first(UN):
                    dve.wait_ge(out_stored[t.slot], t.turn(16))
                dve.tensor_reduce(YS[:, t.odd, :], YT[:, t.slot].rearrange("p k d -> p d k"), AX.X, ALU.add).then_inc(ysum, 1)
                dve.wait_ge(ysum, t.times(1, 1))
                x1 = X1[:, bass.ds(t.times(1), 1), :].rearrange("p t d -> p (t d)")
                dve.tensor_tensor(OUT[:, t.slot, :], YS[:, t.odd, :], x1, ALU.add).then_inc(out_ready, 1)

            for j in range(UN):
                total(Step(j))
            with dve.Fori(0, NT // UN - 1) as i:
                for j in range(UN):
                    total(Step(UN + j, i, UN))

        @block.gpsimd
        def _(pool):
            count = [0]

            def link(ins):
                count[0] += 1
                ins.then_inc(cst, 1)
                pool.wait_ge(cst, count[0])

            link(pool.memset(ident[:, :], 0.0))
            link(pool.affine_select(out=ident[:, :], in_=ident[:, :], compare_op=ALU.not_equal, fill=1.0, base=0,
                                    pattern=[[-1, P]], channel_multiplier=1))
            link(pool.memset(tri[:, :], 1.0))
            link(pool.affine_select(out=tri[:, :], in_=tri[:, :], compare_op=ALU.is_gt, fill=0.0, base=0,
                                    pattern=[[1, P]], channel_multiplier=-1))
            link(pool.memset(mask[:, :, :, :], 0.0))
            for e in range(2):
                for t in range(2):
                    for k in range(NB):
                        mk = mask[e * BLK:(e + 1) * BLK, t, k, 0:WK]
                        link(pool.affine_select(out=mk, in_=mk, compare_op=ALU.is_gt, fill=NEG, base=0,
                                                pattern=[[1, WK]], channel_multiplier=-1))
                        link(pool.affine_select(out=mk, in_=mk, compare_op=ALU.is_ge, fill=NEG, base=WIN,
                                                pattern=[[-1, WK]], channel_multiplier=1))
            link(pool.memset(mask[:, 0, 0, 0:WIN], NEG))
            link(pool.iota(token_id[:, :], pattern=[[P, NT]], base=0, channel_multiplier=1))
            link(pool.iota(iota_e[:, :], pattern=[[1, EX]], base=0, channel_multiplier=0,
                           allow_small_or_imprecise_dtypes=True))
            link(pool.iota(result_row[:, :, :], pattern=[[P * TOPK, NT], [1, TOPK]], base=-BIG,
                           channel_multiplier=TOPK, allow_small_or_imprecise_dtypes=True))
            link(pool.memset(init_i[:, :], T))
            link(pool.memset(zero[:, :], 0.0))
            pool.memset(init_row[:, :], -1.0).then_inc(init_done, 1)
            for q in range(4):
                n = NT // 4
                pool.wait_ge(xa_ready, n * (q + 1))
                pool.tensor_tensor(X1[:, q * n:(q + 1) * n, :], X1[:, q * n:(q + 1) * n, :], XA[:, q * n:(q + 1) * n, :],
                                   ALU.add).then_inc(res_ready, 1)

            class PoolChain:

                def __init__(self, d):
                    self.d, self.n = d, 0

                def __call__(self, ins):
                    self.n += 1
                    ins.then_inc(pool_d, 1)
                    hold(pool, pool_d, self.d.times(NP, self.n))

            def step(s):
                if has_d(s):
                    d = s - 3
                    hold(pool, pos_evac, d.times(1, 1))
                    lp = PoolChain(d)
                    lp(pool.tensor_tensor(hotp[:, :, :], hot[:, :, :],
                                          place[:, :].unsqueeze(1).broadcast_to([P, TOPK, EX]), ALU.mult))
                    lp(pool.tensor_tensor(Macc[:, :], Macc[:, :], M[:, :], ALU.add))
                    w = EX // 2
                    while w:
                        lp(pool.tensor_tensor(hotp[:, :, 0:w], hotp[:, :, 0:w], hotp[:, :, w:2 * w], ALU.add))
                        w //= 2
                    pos = hotp[:, :, 0]
                    lp(pool.tensor_scalar(over[:, :], pos, float(BIG), float(BIG * (CAP - 1)), ALU.mult, ALU.max))
                    lp(pool.tensor_tensor(over[:, :], over[:, :], pos, ALU.add))
                    if not d.first(2):
                        hold(pool, slot_stored[d.odd], d.turn(96, ring=2))
                    lp(pool.tensor_copy(tid[:, d.odd:d.odd + 1], token_id[:, bass.ds(d.times(1), 1)]))
                    lp(pool.tensor_tensor(over[:, :], over[:, :], slotf[:, d.odd, :], ALU.add))
                    pool.tensor_copy(slot[:, d.odd, :], over[:, :]).then_inc(slot_ready, 1)
                    hold(pool, slot_ready, d.times(1, 1))
                    assert lp.n == NP
                    for k in range(TOPK):
                        pool.indirect_dma_start(table, bass.IndirectOffsetOnAxis(ap=slot[:, d.odd, k:k + 1], axis=0),
                                                tid[:, d.odd:d.odd + 1], None, bounds_check=EX * CAP - 1,
                                                oob_is_err=False).then_inc(slot_stored[d.odd], 16)

            pool.wait_ge(table_init, 32)
            steps(pool, step)
            for t in range(2):
                pool.wait_ge(slot_stored[t], 96 * NT // 2)
                pool.wait_ge(row_stored[t], 16 * NT // 2)
            pool.sem_inc(routed, 1)
            pool.wait_ge(tab_ready, 1)
            most = pool.value_load(cmax[0:1, 0:1], min_val=0, max_val=T)

            def experts(base, nt, first):
                def gather(e):
                    if base or not e.first(UN):
                        hold(pool, et_done, e.times(1, base + 1 - UN))
                        hold(pool, idx_ready, e.times(1, base + 1 - UN))
                    pool.tensor_copy(gidx[:, e.slot, 0:nt],
                                     tabT[:, bass.ds(e.times(1), 1), first:first + nt].rearrange("p e t -> p (e t)"))\
                        .then_inc(idx_free, 1)
                    hold(pool, idx_free, e.times(1, base + 1))
                    for t in range(nt):
                        pool.indirect_dma_start(XG[:, e.slot, t, :], None, rows,
                                                bass.IndirectOffsetOnAxis(ap=gidx[:, e.slot, t:t + 1], axis=0),
                                                bounds_check=T, oob_is_err=False).then_inc(xg_loaded[e.slot], 16)

                def scatter(e):
                    hold(pool, y_ready, e.times(1, base + 1))
                    hold(pool, idx_ready, e.times(1, base + 1))
                    for t in range(nt):
                        pool.indirect_dma_start(results, bass.IndirectOffsetOnAxis(ap=dest[:, e.slot, t:t + 1], axis=0),
                                                YE[:, e.slot, t, :], None, bounds_check=T * TOPK - 1,
                                                oob_is_err=False).then_inc(y_stored[e.slot], 16)

                def step(e):
                    if e.i is not None or e.off + UN < EX:
                        gather(e + UN)
                    if not base and e.first():
                        pool.wait_ge(all_stored, 1)
                    scatter(e)

                for j in range(UN):
                    gather(Step(j))
                in_flight(pool, step)

            n0 = MAIN // P
            experts(0, n0, 0)
            for j in range(UN):
                pool.wait_ge(y_stored[j], 16 * n0 * EX // UN)
            with pool.If(most > MAIN):
                n1 = TPE - n0
                experts(EX, n1, n0)
                for j in range(UN):
                    pool.wait_ge(y_stored[j], 16 * (n0 + n1) * EX // UN)
                pool.sem_inc(all_stored, 1)
            with pool.Else():
                pool.sem_inc(all_stored, 1)


def kernel(**inputs):
    import numpy as _np
    import concourse.bacc as _bacc
    from concourse import mybir as _mybir
    from concourse.bass_utils import run_bass_kernel_spmd as _run

    a = {k: _np.asarray(v) for k, v in inputs.items()}
    wg = a["L0_ffn_w_gate"].transpose(0, 2, 1)
    wu = a["L0_ffn_w_up"].transpose(0, 2, 1)
    w1 = _np.zeros((EX, D, W1C), wg.dtype)
    w1[:, :, 0:P] = wg[:, :, 0:P]
    w1[:, :, P:2 * P] = wu[:, :, 0:P]
    w1[:, :, 2 * P:2 * P + FT] = wg[:, :, P:F]
    w1[:, :, 2 * P + 64:W1C] = wu[:, :, P:F]
    data = [
        ("x", a["L0_attn_x"].reshape(T, D)), ("glob", a["L0_attn_global_tokens"].reshape(G, D).T),
        ("ln_s", a["L0_attn_ln_scale"].reshape(DC, P).T), ("ln_b", a["L0_attn_ln_bias"].reshape(DC, P).T),
        ("wq", a["L0_attn_Wq"].T), ("wk", a["L0_attn_Wk"].T), ("wv", a["L0_attn_Wv"].T), ("wo", a["L0_attn_Wo"].T),
        ("gate", a["L0_ffn_gate_w"].T),
        ("w1", w1.reshape(EX, DC, P, W1C).transpose(0, 2, 1, 3)),
        ("w2", a["L0_ffn_w_down"].transpose(0, 2, 1)),
        ("shg", a["L0_ffn_sh_gate"].T), ("shu", a["L0_ffn_sh_up"].T), ("shd", a["L0_ffn_sh_down"].T),
    ]
    nc = _bacc.Bacc("TRN2", target_bir_lowering=False, num_devices=1)
    arrays, args = {}, []
    for name, v in data:
        v = _np.ascontiguousarray(v)
        arrays[f"in_{name}"] = v
        args.append(nc.dram_tensor(f"in_{name}", v.shape, _mybir.dt.from_np(v.dtype), kind="ExternalInput").ap())
    args.append(nc.dram_tensor("out", (T, D), F32, kind="ExternalOutput").ap())
    build(nc, *args)
    r = _run(nc, [arrays], core_ids=[0])
    return r.results[0]["out"].reshape(1, T, D)
```
